# Optimizing a Trainium2 kernel written in Bass

```python
import numpy as np
import jax
import jax.numpy as jnp

def _softmax(x, axis=-1):
    return jax.nn.softmax(x, axis=axis)

def _gelu(x):
    return jax.nn.gelu(x, approximate=True)

def _silu(x):
    return jax.nn.silu(x)

def _sigmoid(x):
    return jax.nn.sigmoid(x)

def _layernorm(x, axis=-1, eps=1e-05):
    m = jnp.mean(x, axis=axis, keepdims=True)
    v = jnp.var(x, axis=axis, keepdims=True)
    return (x - m) / jnp.sqrt(v + eps)

def _scatter_add(tgt, idx, src, axis=0):
    return tgt.at[idx].add(src)

def _segment_sum(src, seg, n):
    return jax.ops.segment_sum(src, seg, n)
kernel_name = 'mk_cond_resid_d2_seqx_r8_5d1e61'

def setup_inputs(seed: int=0):
    np.random.seed(seed)
    _w = jnp.asarray

    def _rec_inputs():
        import jax
        import jax.numpy as jnp
        _rk = jax.random.key(seed)
        x = -0.0005207 + 1.001 * jax.random.normal(jax.random.fold_in(_rk, 1), (32, 32, 512), jnp.float32)
        _lenS = 32 - jax.random.randint(jax.random.fold_in(_rk, 7), (32,), 0, max(1, 32 // 4) + 1, jnp.int32)
        _lenS2 = 32 - jax.random.randint(jax.random.fold_in(_rk, 8), (32,), 0, max(1, 32 // 4) + 1, jnp.int32)
        itok_Bx16_0_63 = jax.random.randint(jax.random.fold_in(_rk, 11), (32, 16), 0, 64, jnp.int32)
        itok_B_207_1644 = jax.random.randint(jax.random.fold_in(_rk, 12), (32,), 207, 1645, jnp.int32)
        itok_B_0_7 = jax.random.randint(jax.random.fold_in(_rk, 13), (32,), 0, 8, jnp.int32)
        return (x, itok_Bx16_0_63, itok_B_207_1644, itok_B_0_7)
    x, itok_Bx16_0_63, itok_B_207_1644, itok_B_0_7 = _rec_inputs()

    def _L0_cond_setup():
        import jax, jax.numpy as jnp
        import numpy as np
        B, S, HID = (4, 128, 512)
        D, HQ, HK = (128, 32, 8)
        PAGES, PSIZE, NPP = (64, 32, 16)
        THETA = 10000.0
        EPS = 1e-06
        SCALE = 1.0 / float(np.sqrt(D))

        def _rmsnorm(t, w):
            var = jnp.mean(t * t, axis=-1, keepdims=True)
            return t * jax.lax.rsqrt(var + EPS) * w

        def _rope(t, pos):
            inv_freq = 1.0 / THETA ** (jnp.arange(0, D, 2, dtype=jnp.float32) / D)
            freqs = pos[..., None].astype(jnp.float32) * inv_freq
            cos = jnp.cos(freqs)[:, :, None, :]
            sin = jnp.sin(freqs)[:, :, None, :]
            t1, t2 = (t[..., :D // 2], t[..., D // 2:])
            return jnp.concatenate([t1 * cos - t2 * sin, t2 * cos + t1 * sin], axis=-1)
        key = jax.random.key(seed)
        ks = jax.random.split(key, 10)
        x = jax.random.normal(ks[0], (B, S, HID), jnp.float32)
        Wq = jax.random.normal(ks[1], (HQ * D, HID), jnp.float32) * 0.02
        Wk = jax.random.normal(ks[2], (HK * D, HID), jnp.float32) * 0.02
        Wv = jax.random.normal(ks[3], (HK * D, HID), jnp.float32) * 0.02
        Wo = jax.random.normal(ks[4], (HID, HQ * D), jnp.float32) * 0.02
        q_norm_w = jax.random.uniform(ks[5], (D,), jnp.float32)
        k_norm_w = jax.random.uniform(ks[6], (D,), jnp.float32)
        k_cache = jax.random.normal(ks[7], (PAGES, PSIZE, HK, D), jnp.float32)
        v_cache = jax.random.normal(ks[8], (PAGES, PSIZE, HK, D), jnp.float32)
        block_table = jnp.arange(B * NPP, dtype=jnp.int32).reshape(B, NPP)
        cache_seqlens = jax.random.randint(ks[9], (B,), 0, 475).astype(jnp.int32)
        return dict(x=x, Wq=Wq, Wk=Wk, Wv=Wv, Wo=Wo, q_norm_w=q_norm_w, k_norm_w=k_norm_w, k_cache=k_cache, v_cache=v_cache, block_table=block_table, cache_seqlens=cache_seqlens)
    _L0_cond_all = _L0_cond_setup()
    _L0_cond_in = {k: v for k, v in _L0_cond_all.items() if k in ('Wq', 'Wk', 'Wv', 'Wo', 'q_norm_w', 'k_norm_w', 'k_cache', 'v_cache')}
    del _L0_cond_all

    def _L1_cond_setup():
        import jax, jax.numpy as jnp
        import numpy as np
        TOP_K = 2
        LANG_BIAS = 5.0
        SCALING = 32.0 / 16.0
        LANGUAGE_PAD_ID = -1
        key = jax.random.key(seed)
        ks = jax.random.split(key, 6)
        B, T, D, O, E, R = (4, 256, 512, 512, 8, 16)
        x = jax.random.normal(ks[0], (B, T, D), dtype=jnp.float32)
        language_ids = jax.random.randint(ks[1], (B,), 0, E).astype(jnp.int64)
        W = jax.random.normal(ks[2], (O, D), dtype=jnp.float32) * (1.0 / np.sqrt(D))
        Wr = jax.random.normal(ks[3], (E, D), dtype=jnp.float32) * (1.0 / np.sqrt(D))
        A = jax.random.normal(ks[4], (E, R, D), dtype=jnp.float32) * (1.0 / np.sqrt(D))
        Bm = jax.random.normal(ks[5], (O, R), dtype=jnp.float32) * 0.0
        Bm = jnp.broadcast_to(Bm, (E, O, R)) + jax.random.normal(ks[5], (E, O, R), dtype=jnp.float32) * 0.02
        return {'x': x, 'language_ids': language_ids, 'W': W, 'Wr': Wr, 'A': A, 'B': Bm}
    _L1_cond_all = _L1_cond_setup()
    _L1_cond_in = {k: v for k, v in _L1_cond_all.items() if k in ('W', 'Wr', 'A', 'B')}
    del _L1_cond_all
    return {'x': x, 'itok_Bx16_0_63': itok_Bx16_0_63, 'itok_B_207_1644': itok_B_207_1644, 'itok_B_0_7': itok_B_0_7, 'L0_cond_Wq': _L0_cond_in['Wq'], 'L0_cond_Wk': _L0_cond_in['Wk'], 'L0_cond_Wv': _L0_cond_in['Wv'], 'L0_cond_Wo': _L0_cond_in['Wo'], 'L0_cond_q_norm_w': _L0_cond_in['q_norm_w'], 'L0_cond_k_norm_w': _L0_cond_in['k_norm_w'], 'L0_cond_k_cache': _L0_cond_in['k_cache'], 'L0_cond_v_cache': _L0_cond_in['v_cache'], 'L1_cond_W': _L1_cond_in['W'], 'L1_cond_Wr': _L1_cond_in['Wr'], 'L1_cond_A': _L1_cond_in['A'], 'L1_cond_B': _L1_cond_in['B']}

def reference(x, itok_Bx16_0_63, itok_B_207_1644, itok_B_0_7, L0_cond_Wq, L0_cond_Wk, L0_cond_Wv, L0_cond_Wo, L0_cond_q_norm_w, L0_cond_k_norm_w, L0_cond_k_cache, L0_cond_v_cache, L1_cond_W, L1_cond_Wr, L1_cond_A, L1_cond_B):
    import jax
    import jax.numpy as jnp

    def _L0_cond_ref(x, Wq, Wk, Wv, Wo, q_norm_w, k_norm_w, k_cache, v_cache, block_table, cache_seqlens):
        import jax, jax.numpy as jnp
        import numpy as np
        B, S, HID = (4, 128, 512)
        D, HQ, HK = (128, 32, 8)
        PAGES, PSIZE, NPP = (64, 32, 16)
        THETA = 10000.0
        EPS = 1e-06
        SCALE = 1.0 / float(np.sqrt(D))

        def _rmsnorm(t, w):
            var = jnp.mean(t * t, axis=-1, keepdims=True)
            return t * jax.lax.rsqrt(var + EPS) * w

        def _rope(t, pos):
            inv_freq = 1.0 / THETA ** (jnp.arange(0, D, 2, dtype=jnp.float32) / D)
            freqs = pos[..., None].astype(jnp.float32) * inv_freq
            cos = jnp.cos(freqs)[:, :, None, :]
            sin = jnp.sin(freqs)[:, :, None, :]
            t1, t2 = (t[..., :D // 2], t[..., D // 2:])
            return jnp.concatenate([t1 * cos - t2 * sin, t2 * cos + t1 * sin], axis=-1)
        bsz, seqlen, _ = x.shape
        q = jnp.einsum('bsd,ed->bse', x, Wq).reshape(bsz, seqlen, HQ, D)
        k = jnp.einsum('bsd,ed->bse', x, Wk).reshape(bsz, seqlen, HK, D)
        v = jnp.einsum('bsd,ed->bse', x, Wv).reshape(bsz, seqlen, HK, D)
        q = _rmsnorm(q, q_norm_w)
        k = _rmsnorm(k, k_norm_w)
        pos = cache_seqlens[:, None] + jnp.arange(seqlen)[None, :]
        q = _rope(q, pos)
        k = _rope(k, pos)
        L = NPP * PSIZE
        kc = k_cache[block_table].reshape(bsz, L, HK, D)
        vc = v_cache[block_table].reshape(bsz, L, HK, D)
        k_all = jnp.concatenate([kc, k], axis=1)
        v_all = jnp.concatenate([vc, v], axis=1)
        valid_c = jnp.arange(L)[None, :] < cache_seqlens[:, None]
        valid = jnp.concatenate([valid_c, jnp.ones((bsz, seqlen), dtype=bool)], axis=1)
        rep = HQ // HK
        k_all = jnp.repeat(k_all, rep, axis=2)
        v_all = jnp.repeat(v_all, rep, axis=2)
        scores = jnp.einsum('bqhd,bkhd->bhqk', q, k_all) * SCALE
        scores = jnp.where(valid[:, None, None, :], scores, -1e+30)
        probs = jax.nn.softmax(scores, axis=-1)
        o = jnp.einsum('bhqk,bkhd->bqhd', probs, v_all)
        o = o.reshape(bsz, seqlen, HQ * D)
        return jnp.einsum('bse,de->bsd', o, Wo)

    def _L1_cond_ref(x, language_ids, W, Wr, A, B):
        import jax, jax.numpy as jnp
        import numpy as np
        TOP_K = 2
        LANG_BIAS = 5.0
        SCALING = 32.0 / 16.0
        LANGUAGE_PAD_ID = -1
        base = jnp.einsum('btd,od->bto', x, W)
        E = Wr.shape[0]
        logits = jnp.einsum('btd,ed->bte', x.astype(jnp.float32), Wr.astype(jnp.float32))
        expert_targets = language_ids
        valid = expert_targets >= 0
        tgt = jnp.where(valid, expert_targets, 0)
        bias = jax.nn.one_hot(tgt, E, dtype=logits.dtype) * LANG_BIAS
        bias = jnp.where(valid[:, None], bias, 0.0)
        logits = logits + bias[:, None, :]
        topw, topi = jax.lax.top_k(logits, TOP_K)
        weights = jax.nn.softmax(topw, axis=-1)
        gates = jnp.sum(jax.nn.one_hot(topi, E, dtype=weights.dtype) * weights[..., None], axis=-2)
        gates = gates.astype(x.dtype)
        h = jnp.einsum('btd,erd->bter', x, A)
        lora_out = jnp.einsum('bter,bte,eor->bto', h, gates, B)
        return base + SCALING * lora_out
    x = x + _L0_cond_ref(x, L0_cond_Wq, L0_cond_Wk, L0_cond_Wv, L0_cond_Wo, L0_cond_q_norm_w, L0_cond_k_norm_w, L0_cond_k_cache, L0_cond_v_cache, itok_Bx16_0_63, itok_B_207_1644)
    x = x + _L1_cond_ref(x, itok_B_0_7, L1_cond_W, L1_cond_Wr, L1_cond_A, L1_cond_B)
    return x

_drawn_inputs = setup_inputs


def setup_inputs(seed=0):
    import zlib

    import numpy as np

    out = dict(_drawn_inputs(seed))
    spreads = {}
    factors = {'L0_cond_Wk': 8.0,
     'L0_cond_Wv': 8.0,
     'L0_cond_k_norm_w': 8.0,
     'L1_cond_Wr': 5.696,
     'L0_cond_k_cache': 4.09,
     'L0_cond_v_cache': 2.928}
    for name, (base, spread) in spreads.items():
        noise = np.random.default_rng([zlib.crc32(name.encode()), seed]).standard_normal(out[name].shape)
        drawn = base * np.exp(spread * noise) if base else spread * noise
        out[name] = jnp.asarray(drawn.astype(out[name].dtype))
    for name, factor in factors.items():
        out[name] = (out[name] * factor).astype(out[name].dtype)
    return out
```

```python
from contextlib import ExitStack

import concourse.bass as bass
from concourse import mybir

ALU = mybir.AluOpType
ACT = mybir.ActivationFunctionType
AX = mybir.AxisListType
F32 = mybir.dt.float32
F32R = mybir.dt.float32r
I32 = mybir.dt.int32
BF16 = mybir.dt.bfloat16

P = 128
BATCH, SEQ, HID = 32, 32, 512
D, HQ, HK = 128, 32, 8
PAGES, PSIZE, NPP = 64, 32, 16
L = NPP * PSIZE
REP = HQ // HK
GK = 2
GROUPS = HK // GK
TILES = BATCH * SEQ // P
ROWS = P // SEQ
PAIRS = ROWS * GK
KC = HID // P
LC = L // P
PPC = P // PSIZE
KEYS = L + P
NBLK = 3
GQ = GK * REP
TOKENS_CACHED = PAGES * PSIZE
SCALE = 1.0 / float(D) ** 0.5
EPS = 1e-6
BIG = 1e30
E_, R_ = 8, 16
ER = E_ * R_
MAGIC = 12582912.0
TWO_PI_1, TWO_PI_2, TWO_PI_3 = 6.28125, 0.0019350051879882812, 3.019916050561733e-07
PI_LOW = 3.1415925


def walk(eng, body):
    def group(g, final):
        body(g, 0, final)
        with eng.Fori(1, TILES - 2) as t:
            body(g, t, final)
        body(g, TILES - 2, final)
        body(g, TILES - 1, final)

    with eng.Fori(0, GROUPS - 1) as g:
        group(g, False)
    group(GROUPS - 1, True)


def program(nc, xT, x, kv, wqkv, wo, block_table, seqlens, lang, qw, kw, inv_freq, w1T, aT, bT, out, y_dram):
    ctx = ExitStack()
    with ctx:
        sb = lambda n, s, d=F32: ctx.enter_context(nc.sbuf_tensor(n, s, d))
        pb = lambda n, s: ctx.enter_context(nc.psum_tensor(n, s, F32))
        sem = lambda n: ctx.enter_context(nc.semaphore(n))

        w_hi = sb("w_hi", [P, NBLK, KC, 512], F32R)
        w_lo = sb("w_lo", [P, NBLK, KC, 512], F32R)
        wo_hi = sb("wo_hi", [P, GQ, HID], F32R)
        wo_lo = sb("wo_lo", [P, GQ, HID], F32R)
        stage = sb("stage", [P, 2, KC, 512])
        x_raw = sb("x_raw", [P, KC, P])
        x_hi = sb("x_hi", [P, KC, P], F32R)
        x_lo = sb("x_lo", [P, KC, P], F32R)
        raw = sb("raw", [P, 512])
        rope_u = sb("rope_u", [P, 512])
        rope_v = sb("rope_v", [P, 512])
        squares = sb("squares", [P, 512], BF16)
        sumsq = sb("sumsq", [P, NBLK, REP])
        meansq = sb("meansq", [P, REP])
        rstd = sb("rstd", [P, REP])
        q_rot = sb("q_rot", [P, GK, 512])
        k_rot = sb("k_rot", [P, GK * D])
        v_next = sb("v_next", [P, GK * D])
        v_new = sb("v_new", [P, GK * D])
        kT_new = sb("kT_new", [P, GK * P])
        qT = sb("qT", [P, GK, ROWS, REP, SEQ])
        kv_rows = sb("kv_rows", [P, ROWS, LC, 2 * GK * D])
        kT = sb("kT", [P, L])
        s_new = sb("s_new", [P, PAIRS, SEQ])
        min_new = sb("min_new", [P, PAIRS])
        scores = sb("scores", [P, ROWS, KEYS])
        min_all = sb("min_all", [P, PAIRS])
        probs = sb("probs", [P, KEYS])
        den = sb("den", [P, PAIRS])
        rden = sb("rden", [P, PAIRS])
        pT = sb("pT", [P, KEYS])
        oT_hi = sb("oT_hi", [P, GQ, P], F32R)
        oT_lo = sb("oT_lo", [P, GQ, P], F32R)
        mask = sb("mask", [P, 2, L])
        y_tile = sb("y_tile", [P, HID])
        ident = sb("ident", [P, P])
        key_index = sb("key_index", [P, L])
        cos = sb("cos", [P, TILES, D // 2])
        sin = sb("sin", [P, TILES, D // 2])
        table = sb("table", [P, 4, D])
        norm_w = sb("norm_w", [P, 2, D])
        warm = sb("warm", [P, 1])
        minus_half = sb("minus_half", [P, REP])
        freq = sb("freq", [P, D // 2])
        seq_i = sb("seq_i", [P, BATCH], I32)
        seq_f = sb("seq_f", [P, BATCH])
        lang_i = sb("lang_i", [P, BATCH], I32)
        lang_f = sb("lang_f", [P, BATCH])
        pos = sb("pos", [P, TILES])
        in_page = sb("in_page", [P, 1])
        lang_t = sb("lang_t", [P, TILES])
        rows_idx = sb("rows_idx", [P, GROUPS, BATCH * LC], I32)
        step_idx = sb("step_idx", [P, ROWS * LC], I32)
        expert = sb("expert", [P, E_])
        mask_w = sb("mask_w", [P, 2, D])

        S = [pb("S0", [P, 512]), pb("S1", [P, 512])]
        KT = pb("KT", [P, L])
        PT = pb("PT", [P, 1024])
        O = pb("O", [P, 512])
        PROJ = pb("PROJ", [P, 512])
        MISC = pb("MISC", [P, 512])

        names = ("consts_in bt_in ident_ready iota_ready setup trig const_ready idx_ready mask_init "
                 "stage0_in stage1_in w_hi_ready w_lo_ready xT_in x_hi_ready x_ready y_init y_in y_added y_stored "
                 "proj_done raw_ready sq_ready ms_ready pow_ready uv_ready sum_ready rot_ready table_ready "
                 "kT_new_done kT_new_ready q_turned qT_ready snew_done snew_ready v_new_ready "
                 "kT_done kT_ready s_done mask_ready min_ready exp_done rden_ready probs_ready "
                 "pT_done pT_ready pv_done o_hi_ready o_ready y_done "
                 "l1_in l1_hi l1_lo l1_turned l1_thi l1_tlo l1_h l1_hcopy l1_g l1_e l1_gate l1_gh l1_ghT l1_ghThi l1_ghTlo "
                 "l1_base l1_sum l1_out0 l1_out1 trig_w step_idx_ready warm").split()
        sm = {n: sem(n) for n in names}
        kv_in = [sem(f"kv_in{b}") for b in range(ROWS)]

        CREDIT = 1
        credits = [sm[n] for n in ("o_ready", "y_added", "exp_done", "y_done", "pv_done")]

        y_all = kv_rows[:, 0:2, :, :].rearrange("p a c n -> p (a c) n")
        rest = kv_rows[:, 2:4, :, :].rearrange("p a c n -> p (a c n)")
        h_all = rest[:, 0:TILES * (ER + E_)].rearrange("p (t n) -> p t n", t=TILES)
        gh = rest[:, 1088:1088 + TILES * ER].rearrange("p (t n) -> p t n", t=TILES)
        lg = rest[:, 2112:2176].rearrange("p (t e) -> p t e", t=TILES)
        pair_gt = rest[:, 2176:2688].rearrange("p (t e f) -> p t e f", t=TILES, e=E_)
        pair_eq = rest[:, 2688:3200].rearrange("p (t e f) -> p t e f", t=TILES, e=E_)
        lower = rest[:, 3200:3264].rearrange("p (e f) -> p e f", e=E_)
        rank = rest[:, 3264:3328].rearrange("p (t e) -> p t e", t=TILES)
        gate = rest[:, 3328:3392].rearrange("p (t e) -> p t e", t=TILES)
        top = rest[:, 3392:3400]
        total = rest[:, 3400:3408]
        expo = rest[:, 3408:3472].rearrange("p (t e) -> p t e", t=TILES)

        y_rows = y_dram.rearrange("(t p) n -> t p n", p=P)

        def three_pass(out_ps, lhs, rhs, n, first=0, stop_at=None):
            mm = None
            for c in range(first, first + n):
                (ah, al), (bh, bl) = lhs(c), rhs(c)
                for k, (a, b) in enumerate(((ah, bh), (ah, bl), (al, bh))):
                    mm = nc.tensor.matmul(out_ps, a, b, start=(c == 0 and k == 0), stop=(c == stop_at and k == 2))
            return mm

        def l1_down(pe, t):
            pe.wait_ge(sm["l1_tlo"], t + 1)
            if t == 0:
                pe.wait_ge(sm["l1_lo"], 3)
            else:
                pe.wait_ge(sm["l1_hcopy"], t)
            three_pass(PROJ[:, 0:ER + E_], lambda c: (wo_hi[:, t, c * P:(c + 1) * P], wo_lo[:, t, c * P:(c + 1) * P]),
                       lambda c: (w_hi[:, 1, c, 0:ER + E_], w_lo[:, 1, c, 0:ER + E_]), KC, 0, KC - 1
                       ).then_inc(sm["l1_h"], 1)

        BLOCK_AT = (1, 4, 6)
        L1_SUB = 10

        block = ctx.enter_context(nc.Block())

        @block.sync
        def _(sp):
            for s in credits:
                sp.sem_inc(s, CREDIT)

            def load_weights(g, k):
                src = wqkv[bass.ds(g * NBLK + k, 1), :, :] if k < NBLK else wo[bass.ds(g * 2 + k - NBLK, 1), :, :]
                half = k % 2
                sp.dma_start(stage[:, half, :, :], src.rearrange("a p n -> p (a n)").rearrange("p (c n) -> p c n", c=KC)
                             ).then_inc(sm["stage1_in" if half else "stage0_in"], 16)

            sp.dma_start(stage[:, 0, :, :], wqkv[0, :, :].rearrange("p (c n) -> p c n", c=KC)).then_inc(sm["stage0_in"], 16)
            sp.dma_start(stage[:, 1, :, :], wqkv[1, :, :].rearrange("p (c n) -> p c n", c=KC)).then_inc(sm["stage1_in"], 16)
            sp.dma_start(x_raw[:, :, :], xT[0, :, :].rearrange("p (c n) -> p c n", c=KC)).then_inc(sm["xT_in"], 16)
            sp.wait_ge(sm["w_lo_ready"], 1)
            sp.dma_start(stage[:, 0, :, :], wqkv[2, :, :].rearrange("p (c n) -> p c n", c=KC)).then_inc(sm["stage0_in"], 16)
            sp.wait_ge(sm["x_ready"], 1)
            sp.dma_start(x_raw[:, :, :], xT[1, :, :].rearrange("p (c n) -> p c n", c=KC)).then_inc(sm["xT_in"], 16)
            sp.dma_start(y_dram[:, :], x[:, :]).then_inc(sm["y_init"], 16)
            sp.wait_ge(sm["y_init"], 16)

            def body(g, t, final):
                i = g * TILES + t
                sp.dma_start(y_tile[:, :], y_rows[bass.ds(t, 1), :, :].rearrange("a p n -> p (a n)")
                             ).then_inc(sm["y_in"], 16)
                if not (final and isinstance(t, int) and t >= TILES - 2):
                    sp.wait_ge(sm["x_ready"], i + 2)
                    sp.nop(nofuse=True)
                    tn = (t + 2) % TILES if isinstance(t, int) else t + 2
                    sp.dma_start(x_raw[:, :, :], xT[bass.ds(tn, 1), :, :].rearrange("a p n -> p (a n)")
                                 .rearrange("p (c n) -> p c n", c=KC)).then_inc(sm["xT_in"], 16)
                if isinstance(t, int) and t == 0:
                    for k in (3, 4):
                        sp.wait_ge(sm["w_lo_ready"], g * 5 + k - 1)
                        sp.nop(nofuse=True)
                        load_weights(g, k)
                if isinstance(t, int) and t == TILES - 2 and not final:
                    for k in range(NBLK):
                        sp.wait_ge(sm["w_lo_ready"], (g + 1) * 5 + max(k - 1, 0))
                        sp.nop(nofuse=True)
                        load_weights(g + 1, k)
                sp.wait_ge(sm["y_added"], CREDIT + i + 1)
                sp.nop(nofuse=True)
                sp.dma_start(y_rows[bass.ds(t, 1), :, :].rearrange("a p n -> p (a n)"), y_tile[:, :]
                             ).then_inc(sm["y_stored"], 16)
                sp.wait_ge(sm["y_stored"], (i + 1) * 16)
                sp.nop(nofuse=True)

            walk(sp, body)
            sp.dma_start(y_all, y_dram.rearrange("(t p) n -> p t n", p=P)).then_inc(sm["l1_in"], 16)
            sp.wait_ge(sm["w_lo_ready"], GROUPS * 5)
            sp.dma_start(stage[:, 0, :, :], w1T.rearrange("p (c n) -> p c n", c=KC)).then_inc(sm["l1_in"], 16)
            sp.dma_start(stage[:, 1, :, 0:ER + E_], aT.rearrange("p (c n) -> p c n", c=KC)).then_inc(sm["l1_in"], 16)
            sp.dma_start(rope_v[:, :], bT[:, :]).then_inc(sm["l1_in"], 16)
            out_rows = out.rearrange("b s n -> (b s) n").rearrange("(t p) n -> t p n", p=P)
            for t in range(TILES):
                sp.wait_ge(sm["l1_sum"], t + 1)
                sp.dma_start(out_rows[t, :, :], (raw if t % 2 else rope_u)[:, :]).then_inc(sm["l1_out1" if t % 2 else "l1_out0"], 16)
            for s in ("l1_out0", "l1_out1"):
                sp.wait_ge(sm[s], 16 * TILES // 2)

        @block.tensor
        def _(pe):
            xs = lambda c: (x_hi[:, c, :], x_lo[:, c, :])

            def proj(i, k, part, wcount):
                first, n = part
                if first == 0:
                    if k == 0:
                        pe.wait_ge(sm["x_ready"], i + 1)
                        pe.wait_ge(sm["snew_ready"], i * 2)
                    pe.wait_ge(sm["raw_ready"], i * NBLK + k)
                    pe.wait_ge(sm["w_lo_ready"], wcount + k + 1)
                mm = three_pass(PROJ[:, :], xs, lambda c: (w_hi[:, k, c, :], w_lo[:, k, c, :]), n, first, KC - 1)
                if first + n == KC:
                    mm.then_inc(sm["proj_done"], 1)

            def turn_k(i):
                pe.wait_ge(sm["rot_ready"], i * NBLK + 1)
                for h in range(GK):
                    tr = nc.tensor.transpose(MISC[:, h * P:(h + 1) * P], k_rot[:, h * D:(h + 1) * D], ident[:, :])
                tr.then_inc(sm["kT_new_done"], 1)

            def turn_q(i, h):
                pe.wait_ge(sm["rot_ready"], i * NBLK + 2 + h)
                for r in range(REP):
                    tr = nc.tensor.transpose(S[h][:, r * P:(r + 1) * P], q_rot[:, h, r * D:(r + 1) * D], ident[:, :])
                tr.then_inc(sm["q_turned"], 1)

            def new_scores(i):
                pe.wait_ge(sm["qT_ready"], i * GK + GK)
                pe.wait_ge(sm["kT_new_ready"], i + 1)
                pe.wait_ge(sm["raw_ready"], i * NBLK + NBLK)
                for b in range(ROWS):
                    for h in range(GK):
                        p = b * GK + h
                        mm = nc.tensor.matmul(PROJ[:, p * SEQ:(p + 1) * SEQ],
                                              qT[:, h, b, :, :].rearrange("p r s -> p (r s)"),
                                              kT_new[:, h * P + b * SEQ:h * P + (b + 1) * SEQ], start=True, stop=True)
                mm.then_inc(sm["snew_done"], 1)

            def turn_kv(i, p):
                b, h = p // GK, p % GK
                pe.wait_ge(kv_in[b], (i + 1) * 16 * LC)
                for c in range(LC):
                    tr = nc.tensor.transpose(KT[:, c * P:(c + 1) * P], kv_rows[:, b, c, h * D:(h + 1) * D], ident[:, :])
                tr.then_inc(sm["kT_done"], 1)

            def score(i, p):
                b, h = p // GK, p % GK
                pe.wait_ge(sm["kT_ready"], i * PAIRS + p + 1)
                nc.tensor.matmul(S[p % 2][:, :], qT[:, h, b, :, :].rearrange("p r s -> p (r s)"), kT[:, :],
                                 start=True, stop=True).then_inc(sm["s_done"], 1)

            def turn_probs(i, p):
                pe.wait_ge(sm["probs_ready"], i * PAIRS + p + 1)
                for c in range(KEYS // P):
                    tr = nc.tensor.transpose(PT[:, c * P:(c + 1) * P], probs[:, c * P:(c + 1) * P], ident[:, :])
                tr.then_inc(sm["pT_done"], 1)

            def weigh(i, p):
                b, h = p // GK, p % GK
                pe.wait_ge(sm["pT_ready"], i * PAIRS + p + 1)
                pe.wait_ge(sm["o_ready"], CREDIT + i * PAIRS + p)
                if p == 0:
                    pe.wait_ge(sm["v_new_ready"], i + 1)
                for c in range(LC):
                    nc.tensor.matmul(O[:, 0:P], kv_rows[:, b, c, GK * D + h * D:GK * D + (h + 1) * D],
                                     pT[:, c * P:(c + 1) * P], start=c == 0, stop=False)
                nc.tensor.matmul(O[:, 0:P], v_new[:, h * D:(h + 1) * D], pT[:, L:KEYS], start=False, stop=True
                                 ).then_inc(sm["pv_done"], 1)

            def project_out(i, h, wcount):
                if h == 0:
                    pe.wait_ge(sm["y_added"], CREDIT + i)
                    pe.wait_ge(sm["kT_new_ready"], i + 1)
                    pe.wait_ge(sm["w_lo_ready"], wcount)
                pe.wait_ge(sm["o_ready"], CREDIT + i * PAIRS + PAIRS - GK + h + 1)
                mm = three_pass(MISC[:, :], lambda c: (oT_hi[:, c, :], oT_lo[:, c, :]),
                                lambda c: (wo_hi[:, c, :], wo_lo[:, c, :]), REP, h * REP, GQ - 1)
                if h == GK - 1:
                    mm.then_inc(sm["y_done"], 1)

            pe.wait_ge(sm["ident_ready"], 2)
            for k in range(NBLK):
                proj(0, k, (0, KC), 0)
                if k == 0:
                    turn_kv(0, 0)
            turn_k(0)
            for h in range(GK):
                turn_q(0, h)
            new_scores(0)

            def body(g, t, final):
                i = g * TILES + t
                end_of_group = isinstance(t, int) and t == TILES - 1
                last = final and end_of_group
                wcount = g * 5 + (5 if end_of_group else 0)
                fill = [[(0, 0), (0, 1)], [(0, 2), (0, 3)], [(1, 0)], [(1, 1), (1, 2)], [(1, 3)],
                        [(2, 0), (2, 1)], [(2, 2), (2, 3)], []]

                def project_some(n):
                    for k, c in fill[n] if not last else []:
                        proj(i + 1, k, (c, 1), wcount)

                score(i, 0)
                turn_kv(i, 1)
                project_some(0)
                for p in range(PAIRS - 1):
                    score(i, p + 1)
                    turn_probs(i, p)
                    if p + 2 < PAIRS:
                        turn_kv(i, p + 2)
                    elif not last:
                        turn_kv(i + 1, 0)
                    project_some(p + 1)
                    if not last and p == 4:
                        pe.wait_ge(sm["y_added"], CREDIT + i)
                        turn_k(i + 1)
                    weigh(i, p)
                if not last:
                    turn_q(i + 1, 0)
                turn_probs(i, PAIRS - 1)
                project_out(i, 0, g * 5 + 5)
                if not last:
                    turn_q(i + 1, 1)
                weigh(i, PAIRS - 1)
                if not last:
                    new_scores(i + 1)
                project_out(i, 1, g * 5 + 5)

            with pe.Fori(0, GROUPS - 1) as g:
                with pe.Fori(0, TILES - 1) as t:
                    body(g, t, False)
                body(g, TILES - 1, False)
            with pe.Fori(0, TILES - 1) as t:
                body(GROUPS - 1, t, True)
            body(GROUPS - 1, TILES - 1, True)

            pe.wait_ge(sm["l1_in"], 64)
            for t in range(TILES):
                if t >= 2:
                    pe.wait_ge(sm["l1_tlo"], t - 1)
                for c in range(KC):
                    tr = nc.tensor.transpose(S[t % 2][:, c * P:(c + 1) * P], y_all[:, t, c * P:(c + 1) * P], ident[:, :])
                tr.then_inc(sm["l1_turned"], 1)
                if t:
                    l1_down(pe, t - 1)
            l1_down(pe, TILES - 1)
            for t in range(TILES):
                if t >= 2:
                    pe.wait_ge(sm["l1_sum"], t - 1)
                three_pass(S[t % 2][:, :], lambda c: (wo_hi[:, t, c * P:(c + 1) * P], wo_lo[:, t, c * P:(c + 1) * P]),
                           lambda c: (w_hi[:, 0, c, :], w_lo[:, 0, c, :]), KC)
                pe.wait_ge(sm["l1_gh"], t + 1)
                if t:
                    pe.wait_ge(sm["l1_ghTlo"], t)
                nc.tensor.transpose(MISC[:, 0:P], gh[:, t, :], ident[:, :]).then_inc(sm["l1_ghT"], 1)
                pe.wait_ge(sm["l1_ghTlo"], t + 1)
                ah, al = x_hi[:, t % 4, :], x_lo[:, t % 4, :]
                bh, bl = w_hi[:, 2, 0, :], w_lo[:, 2, 0, :]
                nc.tensor.matmul(S[t % 2][:, :], ah, bh, start=False, stop=False)
                nc.tensor.matmul(S[t % 2][:, :], ah, bl, start=False, stop=False)
                nc.tensor.matmul(S[t % 2][:, :], al, bh, start=False, stop=True).then_inc(sm["l1_base"], 1)

        @block.scalar
        def _(act):
            act.dma_start(freq[:, :], inv_freq.to_broadcast([P, D // 2])).then_inc(sm["consts_in"], 16)
            act.dma_start(seq_i[:, :], seqlens.to_broadcast([P, BATCH])).then_inc(sm["consts_in"], 16)
            act.dma_start(lang_i[:, :], lang.to_broadcast([P, BATCH])).then_inc(sm["consts_in"], 16)
            act.dma_start(norm_w[:, 0, :], qw.to_broadcast([P, D])).then_inc(sm["consts_in"], 16)
            act.dma_start(norm_w[:, 1, :], kw.to_broadcast([P, D])).then_inc(sm["consts_in"], 16)
            act.dma_start(scores.bitcast(I32)[:, 0, 0:BATCH * NPP], block_table.to_broadcast([P, BATCH * NPP])
                          ).then_inc(sm["bt_in"], 16)

            act.wait_ge(sm["trig"], 1)
            nc.scalar.activation(sin[:, :, :], sin[:, :, :], ACT.Sin).then_inc(sm["const_ready"], 1)
            act.wait_ge(sm["trig"], 2)
            nc.scalar.activation(cos[:, :, :], cos[:, :, :], ACT.Sin).then_inc(sm["const_ready"], 1)

            def take_block(i, k):
                act.wait_ge(sm["sq_ready"], i * NBLK + k)
                act.wait_ge(sm["proj_done"], i * NBLK + k + 1)
                act.wait_ge(sm["uv_ready"], i * NBLK + k)
                if k == 0:
                    nc.scalar.activation(raw[:, 0:GK * D], PROJ[:, 0:GK * D], ACT.Copy)
                    act.wait_ge(sm["v_new_ready"], i)
                    nc.scalar.activation(v_next[:, :], PROJ[:, GK * D:512], ACT.Copy).then_inc(sm["raw_ready"], 1)
                else:
                    nc.scalar.activation(raw[:, :], PROJ[:, :], ACT.Copy).then_inc(sm["raw_ready"], 1)

            def square_block(i, k):
                act.wait_ge(sm["raw_ready"], i * NBLK + k + 1)
                act.wait_ge(sm["ms_ready"], i * NBLK + k)
                n = GK if k == 0 else REP
                for r in range(n):
                    sq = nc.scalar.activation(squares[:, r * D:(r + 1) * D], raw[:, r * D:(r + 1) * D], ACT.Square,
                                              accum_out=sumsq[:, k, r:r + 1])
                sq.then_inc(sm["sq_ready"], 1)

            def take_kT_new(i):
                act.wait_ge(sm["kT_new_done"], i + 1)
                nc.scalar.activation(kT_new[:, :], MISC[:, 0:GK * P], ACT.Copy).then_inc(sm["kT_new_ready"], 1)

            def take_qT(i, h):
                act.wait_ge(sm["q_turned"], i * GK + h + 1)
                nc.scalar.activation(qT[:, h, :, :, :].rearrange("p b r s -> p r b s"),
                                     S[h][:, :].rearrange("p (r b s) -> p r b s", r=REP, b=ROWS), ACT.Copy
                                     ).then_inc(sm["qT_ready"], 1)

            def take_kT(i, p):
                act.wait_ge(sm["kT_done"], i * PAIRS + p + 1)
                nc.scalar.activation(kT[:, :], KT[:, :], ACT.Copy).then_inc(sm["kT_ready"], 1)

            def take_pT(i, p):
                act.wait_ge(sm["pT_done"], i * PAIRS + p + 1)
                nc.scalar.activation(pT[:, :], PT[:, 0:KEYS], ACT.Copy).then_inc(sm["pT_ready"], 1)

            def exponent(i, p):
                act.wait_ge(sm["min_ready"], i * PAIRS + p + 1)
                nc.scalar.activation(probs[:, :], scores[:, p // GK, :], ACT.Exp, bias=min_all[:, p:p + 1],
                                     scale=-1.0, accum_out=den[:, p:p + 1]).then_inc(sm["exp_done"], 1)

            act.wait_ge(sm["setup"], 3)
            nc.scalar.activation(warm[:, :], minus_half[:, 0:1], ACT.Exp).then_inc(sm["warm"], 1)

            for k in range(NBLK):
                take_block(0, k)
                square_block(0, k)
                if k == 0:
                    take_kT(0, 0)
            take_kT_new(0)
            for h in range(GK):
                take_qT(0, h)

            def body(g, t, final):
                i = g * TILES + t
                last = final and isinstance(t, int) and t == TILES - 1
                take_kT(i, 1)
                exponent(i, 0)
                for p in range(PAIRS - 1):
                    if not last and p in BLOCK_AT:
                        take_block(i + 1, BLOCK_AT.index(p))
                        square_block(i + 1, BLOCK_AT.index(p))
                    take_pT(i, p)
                    exponent(i, p + 1)
                    if not last and p == 5:
                        take_kT_new(i + 1)
                    if p + 2 < PAIRS:
                        take_kT(i, p + 2)
                    elif not last:
                        take_kT(i + 1, 0)
                take_pT(i, PAIRS - 1)
                if not last:
                    take_qT(i + 1, 0)
                    take_qT(i + 1, 1)

            with act.Fori(0, GROUPS * TILES - 1) as i:
                body(0, i, False)
            body(GROUPS - 1, TILES - 1, True)

            for t in range(TILES):
                act.wait_ge(sm["l1_turned"], t + 1)
                if t == 0:
                    act.wait_ge(sm["y_done"], CREDIT + GROUPS * TILES)
                nc.scalar.activation(wo_hi[:, t, :], S[t % 2][:, :], ACT.Copy).then_inc(sm["l1_thi"], 1)
                if t:
                    act.wait_ge(sm["l1_h"], t)
                    nc.scalar.activation(h_all[:, t - 1, :], PROJ[:, 0:ER + E_], ACT.Copy).then_inc(sm["l1_hcopy"], 1)
            act.wait_ge(sm["l1_h"], TILES)
            nc.scalar.activation(h_all[:, TILES - 1, :], PROJ[:, 0:ER + E_], ACT.Copy).then_inc(sm["l1_hcopy"], 1)
            act.wait_ge(sm["l1_g"], L1_SUB)
            nc.scalar.activation(expo, lg, ACT.Exp).then_inc(sm["l1_e"], 1)
            for t in range(TILES):
                act.wait_ge(sm["l1_ghT"], t + 1)
                nc.scalar.activation(x_hi[:, t % 4, :], MISC[:, 0:P], ACT.Copy).then_inc(sm["l1_ghThi"], 1)


        @block.vector
        def _(dve):
            V = nc.vector
            count = [0]

            def setup(ins):
                count[0] += 1
                ins.then_inc(sm["setup"], 1)
                dve.wait_ge(sm["setup"], count[0])

            def split_weights(m, dst, half, nth, src=None):
                dve.wait_ge(sm["stage1_in" if half else "stage0_in"], nth * 16)
                V.tensor_copy(dst, stage[:, half, :, :]).then_inc(sm["w_hi_ready"], 1)

            def split_x(i):
                dve.wait_ge(sm["xT_in"], (i + 1) * 16)
                dve.wait_ge(sm["proj_done"], i * NBLK)
                V.tensor_copy(x_hi[:, :, :], x_raw[:, :, :]).then_inc(sm["x_hi_ready"], 1)
                dve.wait_ge(sm["x_hi_ready"], i + 1)
                V.tensor_tensor(x_lo[:, :, :], x_raw[:, :, :], x_hi[:, :, :].bitcast(F32), ALU.subtract
                                ).then_inc(sm["x_ready"], 1)

            def rotate(i, k):
                dve.wait_ge(sm["raw_ready"], i * NBLK + k + 1)
                dve.wait_ge(sm["sum_ready"], i * NBLK + k)
                dve.wait_ge(sm["rot_ready"], i * NBLK + k)
                dve.wait_ge(sm["table_ready"], (i + 1) * 8)
                n, tc = (GK, 2) if k == 0 else (REP, 0)
                w = n * D
                V.tensor_tensor(rope_u[:, 0:w].rearrange("p (r d) -> p r d", d=D), raw[:, 0:w].rearrange("p (r d) -> p r d", d=D),
                                table[:, tc:tc + 1, :].to_broadcast([P, n, D]), ALU.mult)
                r4 = lambda a: a[:, 0:w].rearrange("p (r f d) -> p r f d", r=n, f=2)
                for f in range(2):
                    last = V.tensor_tensor(r4(rope_v)[:, :, f, :], r4(raw)[:, :, 1 - f, :],
                                           table[:, tc + 1:tc + 2, f * 64:(f + 1) * 64].to_broadcast([P, n, 64]), ALU.mult)
                last.then_inc(sm["uv_ready"], 1)

            def take_new_scores(i):
                dve.wait_ge(sm["snew_done"], i + 1)
                src = PROJ[:, 0:PAIRS * SEQ].rearrange("p (a s) -> p a s", a=PAIRS)
                V.tensor_copy(s_new[:, :, :], src).then_inc(sm["snew_ready"], 1)
                V.tensor_reduce(min_new[:, :], src, AX.X, ALU.min).then_inc(sm["snew_ready"], 1)

            def make_mask(row, b):
                V.tensor_scalar(mask[:, b % 2, :], key_index[:, :], seq_f[:, bass.ds(row, 1)], BIG, ALU.is_ge, ALU.mult
                                ).then_inc(sm["mask_ready"], 1)

            def minimum(i, p):
                b = p // GK
                dve.wait_ge(sm["s_done"], i * PAIRS + p + 1)
                dve.wait_ge(sm["exp_done"], CREDIT + i * PAIRS + p)
                if p % GK == 0:
                    dve.wait_ge(sm["mask_ready"], i * ROWS + b + 1)
                if p == 0:
                    dve.wait_ge(sm["snew_ready"], i * 2 + 2)
                dve.nop(nofuse=True)
                V.tensor_copy(scores[:, b, L + b * SEQ:L + (b + 1) * SEQ], s_new[:, p, :])
                V.tensor_tensor_reduce(scores[:, b, 0:L], S[p % 2][:, :], mask[:, b % 2, :], 1.0, min_new[:, p:p + 1],
                                       ALU.add, ALU.min, min_all[:, p:p + 1]).then_inc(sm["min_ready"], 1)

            def normalise(i, p):
                dve.wait_ge(sm["exp_done"], CREDIT + i * PAIRS + p + 1)
                V.reciprocal(rden[:, p:p + 1], den[:, p:p + 1]).then_inc(sm["rden_ready"], 1)
                dve.wait_ge(sm["rden_ready"], i * PAIRS + p + 1)
                V.tensor_scalar(probs[:, :], probs[:, :], rden[:, p:p + 1], None, ALU.mult).then_inc(sm["probs_ready"], 1)

            def take_o(i, p):
                b, h = p // GK, p % GK
                dve.wait_ge(sm["pv_done"], CREDIT + i * PAIRS + p + 1)
                src = O[:, 0:P].rearrange("p (r s) -> p r s", r=REP)
                hi = oT_hi[:, h * REP:(h + 1) * REP, b * SEQ:(b + 1) * SEQ]
                lo = oT_lo[:, h * REP:(h + 1) * REP, b * SEQ:(b + 1) * SEQ]
                V.tensor_copy(hi, src).then_inc(sm["o_hi_ready"], 1)
                dve.wait_ge(sm["o_hi_ready"], i * PAIRS + p + 1)
                V.tensor_tensor(lo, src, hi.bitcast(F32), ALU.subtract).then_inc(sm["o_ready"], 1)

            def add_y(i):
                dve.wait_ge(sm["y_done"], CREDIT + i + 1)
                dve.wait_ge(sm["y_in"], (i + 1) * 16)
                V.tensor_tensor(y_tile[:, :], y_tile[:, :], MISC[:, :], ALU.add).then_inc(sm["y_added"], 1)

            split_weights(0, w_hi[:, 0, :, :], 0, 1)
            split_x(0)
            split_weights(1, w_hi[:, 1, :, :], 1, 1)
            dve.wait_ge(sm["consts_in"], 80)
            dve.wait_ge(sm["iota_ready"], 3)
            setup(V.tensor_copy(seq_f[:, :], seq_i[:, :]))
            setup(V.tensor_copy(lang_f[:, :], lang_i[:, :]))
            setup(V.memset(minus_half[:, :], -0.5))
            per_row = lambda a, j: a[j * SEQ:(j + 1) * SEQ, :].rearrange("p (t j) -> p t j", j=ROWS)[:, :, j]
            for j in range(ROWS):
                setup(V.tensor_copy(pos[j * SEQ:(j + 1) * SEQ, :], per_row(seq_f, j)))
                setup(V.tensor_copy(lang_t[j * SEQ:(j + 1) * SEQ, :], per_row(lang_f, j)))
                setup(V.tensor_scalar(in_page[j * SEQ:(j + 1) * SEQ, :], in_page[j * SEQ:(j + 1) * SEQ, :],
                                      float(-j * SEQ), None, ALU.add))
            dve.wait_ge(sm["bt_in"], 16)
            pages_i = scores.bitcast(I32)[:, 0, 0:BATCH * NPP]
            pages_f = scores[:, 1, 0:BATCH * NPP]
            base = scores[:, 2, 0:BATCH * LC]
            setup(V.tensor_copy(pages_f, pages_i))
            for j in range(PPC):
                q = slice(j * PSIZE, (j + 1) * PSIZE)
                setup(V.tensor_scalar(base[q, :], pages_f[q, :].rearrange("p (a j) -> p a j", j=PPC)[:, :, j],
                                      float(PSIZE), in_page[q, 0:1], ALU.mult, ALU.add))
            for g in range(GROUPS):
                ins = V.tensor_scalar(rows_idx[:, g, :], base, float(g * TOKENS_CACHED), None, ALU.add)
                ins.then_inc(sm["idx_ready"], 1)
            dve.wait_ge(sm["idx_ready"], GROUPS)
            setup(V.tensor_scalar(pos[:, :], pos[:, :], in_page[:, 0:1], None, ALU.add))
            half_d = D // 2
            flat = lambda a, z: a[:, z, :].rearrange("p (t n) -> p t n", t=TILES) if False else a
            ang = scores[:, 0, 0:TILES * half_d].rearrange("p (t n) -> p t n", t=TILES)
            turns = scores[:, 1, 0:TILES * half_d].rearrange("p (t n) -> p t n", t=TILES)
            setup(V.tensor_tensor(ang, pos[:, :].rearrange("p (t a) -> p t a", a=1).to_broadcast([P, TILES, half_d]),
                                  freq[:, :].rearrange("p (a n) -> p a n", a=1).to_broadcast([P, TILES, half_d]), ALU.mult))
            for n, (dst, quarter, add) in enumerate(((sin, 0.0, 0.0), (cos, 0.25, 1.5707963267948966))):
                setup(V.tensor_scalar(turns, ang, 0.15915494309189535, quarter, ALU.mult, ALU.add))
                setup(V.tensor_scalar(turns, turns, MAGIC, None, ALU.add))
                setup(V.tensor_scalar(turns, turns, -MAGIC, None, ALU.add))
                setup(V.scalar_tensor_tensor(dst[:, :, :], turns, -TWO_PI_1, ang, ALU.mult, ALU.add))
                setup(V.scalar_tensor_tensor(dst[:, :, :], turns, -TWO_PI_2, dst[:, :, :], ALU.mult, ALU.add))
                setup(V.scalar_tensor_tensor(dst[:, :, :], turns, -TWO_PI_3, dst[:, :, :], ALU.mult, ALU.add))
                setup(V.tensor_scalar(dst[:, :, :], dst[:, :, :], add, PI_LOW, ALU.add, ALU.min))
                V.tensor_scalar(dst[:, :, :], dst[:, :, :], -PI_LOW, None, ALU.max).then_inc(sm["trig"], 1)
            dve.wait_ge(sm["trig"], 2)
            V.memset(scores[:, :, :], BIG).then_inc(sm["mask_init"], 1)
            dve.wait_ge(sm["mask_init"], 1)
            make_mask(0, 0)
            dve.wait_ge(sm["w_lo_ready"], 1)
            split_weights(2, w_hi[:, 2, :, :], 0, 2)
            for k in range(NBLK):
                rotate(0, k)
            split_x(1)
            take_new_scores(0)

            def body(g, t, final):
                i = g * TILES + t
                fixed = isinstance(t, int)
                last = final and fixed and t == TILES - 1
                tn = 0 if fixed and t == TILES - 1 else t + 1
                minimum(i, 0)
                make_mask(t * ROWS + 1, 1)
                normalise(i, 0)
                for p in range(PAIRS - 1):
                    minimum(i, p + 1)
                    if (p + 1) % GK == 0:
                        b = (p + 1) // GK + 1
                        if b < ROWS:
                            make_mask(t * ROWS + b, b)
                        elif not last:
                            make_mask(tn * ROWS, b)
                    if not last and p in BLOCK_AT:
                        rotate(i + 1, BLOCK_AT.index(p))
                    if fixed and t == 0 and p in (1, 3):
                        n = p // 2
                        dve.wait_ge(sm["y_done"], CREDIT + i)
                        split_weights(0, wo_hi[:, n * KC:(n + 1) * KC, :], 1 - n, (g + 1) * (3 if n else 2))
                    if fixed and t == TILES - 2 and not final and p in BLOCK_AT:
                        k = BLOCK_AT.index(p)
                        dve.wait_ge(sm["proj_done"], (i + 1) * NBLK + k + 1)
                        split_weights(0, w_hi[:, k, :, :], k % 2, (g + 1) * 3 + 1 + k // 2 if k % 2 == 0 else (g + 1) * 2 + 1)
                    normalise(i, p + 1)
                    take_o(i, p)
                if not (final and fixed and t >= TILES - 2):
                    split_x(i + 2)
                take_o(i, PAIRS - 1)
                if not last:
                    take_new_scores(i + 1)
                add_y(i)

            walk(dve, body)

            dve.wait_ge(sm["l1_in"], 64)
            V.tensor_copy(w_hi[:, 0, :, :], stage[:, 0, :, :]).then_inc(sm["l1_hi"], 1)
            V.tensor_copy(w_hi[:, 1, :, 0:ER + E_], stage[:, 1, :, 0:ER + E_]).then_inc(sm["l1_hi"], 1)
            V.tensor_copy(w_hi[:, 2, 0, :], rope_v[:, :]).then_inc(sm["l1_hi"], 1)
            for t in range(TILES):
                dve.wait_ge(sm["l1_thi"], t + 1)
                V.tensor_tensor(wo_lo[:, t, :], S[t % 2][:, :], wo_hi[:, t, :].bitcast(F32), ALU.subtract
                                ).then_inc(sm["l1_tlo"], 1)
            dve.wait_ge(sm["l1_hcopy"], TILES)
            gs = [0]

            def gating(ins):
                gs[0] += 1
                ins.then_inc(sm["l1_g"], 1)
                dve.wait_ge(sm["l1_g"], gs[0])

            te = [P, TILES, E_]
            tee = [P, TILES, E_, E_]
            ex = expert[:, :]
            gating(V.tensor_tensor(gate, ex.rearrange("p (a e) -> p a e", a=1).to_broadcast(te),
                                   lang_t[:, :].rearrange("p (t a) -> p t a", a=1).to_broadcast(te), ALU.is_equal))
            gating(V.scalar_tensor_tensor(lg, gate, 5.0, h_all[:, :, ER:ER + E_], ALU.mult, ALU.add))
            gating(V.tensor_tensor(lower, ex.rearrange("p (a f) -> p a f", a=1).to_broadcast([P, E_, E_]),
                                   ex.rearrange("p (e a) -> p e a", a=1).to_broadcast([P, E_, E_]), ALU.is_lt))
            other = lg.rearrange("p t (a f) -> p t a f", a=1).to_broadcast(tee)
            own = lg.rearrange("p t (e a) -> p t e a", a=1).to_broadcast(tee)
            gating(V.tensor_tensor(pair_gt, other, own, ALU.is_gt))
            gating(V.tensor_tensor(pair_eq, other, own, ALU.is_equal))
            gating(V.tensor_tensor(pair_eq, pair_eq, lower.rearrange("p (a e) f -> p a e f", a=1).to_broadcast(tee), ALU.mult))
            gating(V.tensor_tensor(pair_gt, pair_gt, pair_eq, ALU.add))
            gating(V.tensor_reduce(rank, pair_gt, AX.X, ALU.add))
            gating(V.tensor_reduce(top, lg, AX.X, ALU.max))
            gating(V.tensor_tensor(lg, lg, top.rearrange("p (t a) -> p t a", a=1).to_broadcast(te), ALU.subtract))
            assert gs[0] == L1_SUB
            dve.wait_ge(sm["l1_e"], 1)
            gating(V.scalar_tensor_tensor(gate, rank, 1.5, expo, ALU.is_lt, ALU.mult))
            gating(V.tensor_reduce(total, gate, AX.X, ALU.add))
            gating(V.reciprocal(total, total))
            gating(V.tensor_scalar(total, total, 2.0, None, ALU.mult))
            gating(V.tensor_tensor(gate, gate, total.rearrange("p (t a) -> p t a", a=1).to_broadcast(te), ALU.mult))
            for t in range(TILES):
                V.tensor_tensor(gh[:, t, :].rearrange("p (e r) -> p e r", e=E_),
                                h_all[:, t, 0:ER].rearrange("p (e r) -> p e r", e=E_),
                                gate[:, t, :].rearrange("p (e a) -> p e a", a=1).to_broadcast([P, E_, R_]), ALU.mult
                                ).then_inc(sm["l1_gh"], 1)
            for t in range(TILES):
                dve.wait_ge(sm["l1_ghThi"], t + 1)
                V.tensor_tensor(x_lo[:, t % 4, :], MISC[:, 0:P], x_hi[:, t % 4, :].bitcast(F32), ALU.subtract
                                ).then_inc(sm["l1_ghTlo"], 1)
                dve.wait_ge(sm["l1_base"], t + 1)
                if t >= 2:
                    dve.wait_ge(sm["l1_out1" if t % 2 else "l1_out0"], 16 * (t // 2))
                V.tensor_tensor((raw if t % 2 else rope_u)[:, :], S[t % 2][:, :], y_all[:, t, :], ALU.add
                                ).then_inc(sm["l1_sum"], 1)

        @block.gpsimd
        def _(pool):
            G = nc.gpsimd
            G.memset(ident[:, :], 0.0).then_inc(sm["ident_ready"], 1)
            pool.wait_ge(sm["ident_ready"], 1)
            G.affine_select(out=ident[:, :], in_=ident[:, :], compare_op=ALU.not_equal, fill=1.0, base=0,
                            pattern=[[-1, P]], channel_multiplier=1).then_inc(sm["ident_ready"], 1)
            G.iota(key_index[:, :], [[1, L]], base=0, channel_multiplier=0, allow_small_or_imprecise_dtypes=True
                   ).then_inc(sm["iota_ready"], 1)
            G.iota(in_page[:, :], [[0, 1]], base=0, channel_multiplier=1, allow_small_or_imprecise_dtypes=True
                   ).then_inc(sm["iota_ready"], 1)
            G.iota(expert[:, :], [[1, E_]], base=0, channel_multiplier=0, allow_small_or_imprecise_dtypes=True
                   ).then_inc(sm["iota_ready"], 1)

            def split_rest(m, hi, lo, half, first=None):
                pool.wait_ge(sm["w_hi_ready"], m + 1)
                G.tensor_tensor(lo, stage[:, half, :, :], hi.bitcast(F32), ALU.subtract).then_inc(sm["w_lo_ready"], 1)

            def gather(b, first, n):
                for c in range(first, first + n):
                    G.indirect_dma_start(kv_rows[:, b, c, :], None, kv[:, :],
                                         bass.IndirectOffsetOnAxis(ap=step_idx[:, b * LC + c:b * LC + c + 1], axis=0)
                                         ).then_inc(kv_in[b], 16)

            def take_indices(i, b0, b1, nth):
                pool.nop(nofuse=True)
                G.tensor_copy(step_idx[:, b0 * LC:b1 * LC], idx_flat[:, bass.ds(i * (ROWS * LC) + b0 * LC, (b1 - b0) * LC)]
                              ).then_inc(sm["step_idx_ready"], 1)
                pool.wait_ge(sm["step_idx_ready"], nth)
                pool.nop(nofuse=True)

            idx_flat = rows_idx[:, :, :].rearrange("p g n -> p (g n)")

            def make_table(i, tn):
                pool.wait_ge(sm["uv_ready"], i * NBLK)
                c, s = (a[:, bass.ds(tn, 1), :].rearrange("p a n -> p (a n)") for a in (cos, sin))
                for z, scale in ((0, -SCALE), (1, 1.0)):
                    for f, sign in ((0, -1.0), (1, 1.0)):
                        cols = slice(f * 64, (f + 1) * 64)
                        other = slice((1 - f) * 64, (2 - f) * 64)
                        G.tensor_tensor(table[:, 2 * z, cols], c, weights[z][:, cols], ALU.mult
                                        ).then_inc(sm["table_ready"], 1)
                        G.tensor_tensor(table[:, 2 * z + 1, cols], s, weights_signed[z][:, other], ALU.mult
                                        ).then_inc(sm["table_ready"], 1)

            weights = [norm_w[:, 0, :], norm_w[:, 1, :]]
            weights_signed = [mask_w[:, 0, :], mask_w[:, 1, :]]

            def norm_rotate(i, k):
                n = GK if k == 0 else REP
                nth = i * NBLK + k + 1
                pool.wait_ge(sm["sq_ready"], nth)
                pool.nop(nofuse=True)
                G.tensor_scalar(meansq[:, 0:n], sumsq[:, k, 0:n], 1.0 / D, EPS, ALU.mult, ALU.add
                                ).then_inc(sm["ms_ready"], 1)
                pool.wait_ge(sm["ms_ready"], nth)
                G.tensor_tensor(rstd[:, 0:n], meansq[:, 0:n], minus_half[:, 0:n], ALU.pow).then_inc(sm["pow_ready"], 1)
                pool.wait_ge(sm["uv_ready"], nth)
                w = n * D
                G.tensor_tensor(rope_u[:, 0:w], rope_u[:, 0:w], rope_v[:, 0:w], ALU.add).then_inc(sm["sum_ready"], 1)
                pool.wait_ge(sm["sum_ready"], nth)
                pool.wait_ge(sm["pow_ready"], nth)
                if k == 0:
                    pool.wait_ge(sm["kT_new_done"], i)
                    dst = k_rot[:, :]
                else:
                    pool.wait_ge(sm["q_turned"], i * GK)
                    dst = q_rot[:, k - 1, :]
                G.tensor_tensor(dst.rearrange("p (r d) -> p r d", d=D), rope_u[:, 0:w].rearrange("p (r d) -> p r d", d=D),
                                rstd[:, 0:n].rearrange("p (r a) -> p r a", a=1).to_broadcast([P, n, D]), ALU.mult
                                ).then_inc(sm["rot_ready"], 1)

            def keep_v(i):
                pool.wait_ge(sm["raw_ready"], i * NBLK + 1)
                pool.wait_ge(sm["pv_done"], CREDIT + i * PAIRS)
                pool.nop(nofuse=True)
                G.tensor_copy(v_new[:, :], v_next[:, :]).then_inc(sm["v_new_ready"], 1)

            split_rest(0, w_hi[:, 0, :, :], w_lo[:, 0, :, :], 0)
            split_rest(1, w_hi[:, 1, :, :], w_lo[:, 1, :, :], 1)
            pool.wait_ge(sm["idx_ready"], GROUPS)
            take_indices(0, 0, ROWS - 1, 1)
            for b in range(ROWS - 1):
                gather(b, 0, LC)
            pool.wait_ge(sm["consts_in"], 80)
            G.tensor_scalar(norm_w[:, 0, :], norm_w[:, 0, :], -SCALE, 0.0, ALU.mult, ALU.add).then_inc(sm["trig_w"], 1)
            pool.wait_ge(sm["trig_w"], 1)
            for z in range(2):
                G.tensor_scalar(mask_w[:, z, 0:64], norm_w[:, z, 0:64], 1.0, 0.0, ALU.mult, ALU.add).then_inc(sm["trig_w"], 1)
                G.tensor_scalar(mask_w[:, z, 64:128], norm_w[:, z, 64:128], -1.0, 0.0, ALU.mult, ALU.add).then_inc(sm["trig_w"], 1)
            pool.wait_ge(sm["trig_w"], 5)
            pool.wait_ge(sm["const_ready"], 2)
            make_table(0, 0)
            split_rest(2, w_hi[:, 2, :, :], w_lo[:, 2, :, :], 0)
            for k in range(NBLK):
                norm_rotate(0, k)
            keep_v(0)
            pool.wait_ge(sm["mask_init"], 1)

            def body(g, t, final):
                i = g * TILES + t
                fixed = isinstance(t, int)
                last = final and fixed and t == TILES - 1
                tn = 0 if fixed and t == TILES - 1 else t + 1
                for p in range(PAIRS):
                    if not last and p == 0:
                        make_table(i + 1, tn)
                    if not last and p - 1 in BLOCK_AT:
                        norm_rotate(i + 1, BLOCK_AT.index(p - 1))
                    if p < 2:
                        b = ROWS - 1
                        if p == 0:
                            pool.wait_ge(sm["pv_done"], CREDIT + i * PAIRS)
                            take_indices(i, b, b + 1, 2 * i + 2)
                        gather(b, 2 * p, 2)
                    elif not last:
                        b = p // 2 - 1
                        if p == 2:
                            for row in range(ROWS - 1):
                                pool.wait_ge(kv_in[row], (i + 1) * 16 * LC)
                            take_indices(i + 1, 0, ROWS - 1, 2 * i + 3)
                        pool.wait_ge(sm["pv_done"], CREDIT + i * PAIRS + b * GK + GK)
                        pool.nop(nofuse=True)
                        gather(b, 2 * (p % 2), 2)
                    if fixed and t == 0 and p in (2, 4):
                        n = p // 2 - 1
                        split_rest(g * 5 + 3 + n, wo_hi[:, n * KC:(n + 1) * KC, :], wo_lo[:, n * KC:(n + 1) * KC, :], 1 - n)
                    if fixed and t == TILES - 2 and not final and p in (4, 6, 7):
                        k = {4: 0, 6: 1, 7: 2}[p]
                        split_rest((g + 1) * 5 + k, w_hi[:, k, :, :], w_lo[:, k, :, :], k % 2)
                if not last:
                    keep_v(i + 1)

            walk(pool, body)
            pool.wait_ge(sm["l1_hi"], 3)
            G.tensor_tensor(w_lo[:, 1, :, 0:ER + E_], stage[:, 1, :, 0:ER + E_], w_hi[:, 1, :, 0:ER + E_].bitcast(F32),
                            ALU.subtract).then_inc(sm["l1_lo"], 1)
            G.tensor_tensor(w_lo[:, 0, :, :], stage[:, 0, :, :], w_hi[:, 0, :, :].bitcast(F32), ALU.subtract
                            ).then_inc(sm["l1_lo"], 1)
            G.tensor_tensor(w_lo[:, 2, 0, :], rope_v[:, :], w_hi[:, 2, 0, :].bitcast(F32), ALU.subtract
                            ).then_inc(sm["l1_lo"], 1)


def kernel(x, itok_Bx16_0_63, itok_B_207_1644, itok_B_0_7, L0_cond_Wq, L0_cond_Wk, L0_cond_Wv, L0_cond_Wo,
           L0_cond_q_norm_w, L0_cond_k_norm_w, L0_cond_k_cache, L0_cond_v_cache, L1_cond_W, L1_cond_Wr, L1_cond_A, L1_cond_B):
    import numpy as np
    import concourse.bacc as bacc
    from concourse.bass_utils import run_bass_kernel_spmd

    def chunked(wT):
        return np.asarray(wT).reshape(KC, P, -1).transpose(1, 0, 2).reshape(P, -1)

    x2 = np.asarray(x).reshape(BATCH * SEQ, HID)
    xT = x2.reshape(TILES, P, KC, P).transpose(0, 3, 2, 1).reshape(TILES, P, KC * P)
    k4 = np.asarray(L0_cond_k_cache).reshape(TOKENS_CACHED, GROUPS, GK * D)
    v4 = np.asarray(L0_cond_v_cache).reshape(TOKENS_CACHED, GROUPS, GK * D)
    kv = np.concatenate([k4, v4], axis=2).transpose(1, 0, 2).reshape(GROUPS * TOKENS_CACHED, 2 * GK * D)
    wq, wk, wv, wo = (np.asarray(a) for a in (L0_cond_Wq, L0_cond_Wk, L0_cond_Wv, L0_cond_Wo))
    blocks = []
    for g in range(GROUPS):
        n = GK * D
        blocks.append(chunked(np.concatenate([wk[g * n:(g + 1) * n], wv[g * n:(g + 1) * n]], axis=0).T))
        for h in range(GK):
            r = (g * GK + h) * REP * D
            blocks.append(chunked(wq[r:r + REP * D].T))
    wo_l = wo.T.reshape(GROUPS * 2, REP, D, HID).transpose(0, 2, 1, 3).reshape(GROUPS * 2, D, REP * HID)
    a_all = np.concatenate([np.asarray(L1_cond_A).reshape(ER, HID), np.asarray(L1_cond_Wr)], axis=0)
    exponents = np.arange(0, D, 2, dtype=np.float32) / np.float32(D)
    inv_freq = np.float32(1.0) / np.power(10000.0, exponents.astype(np.float64)).astype(np.float32)
    ins = dict(
        xT=xT, x=x2, kv=kv, wqkv=np.stack(blocks), wo=wo_l,
        block_table=np.asarray(itok_Bx16_0_63).reshape(1, -1), seqlens=np.asarray(itok_B_207_1644).reshape(1, -1),
        lang=np.asarray(itok_B_0_7).reshape(1, -1), qw=np.asarray(L0_cond_q_norm_w).reshape(1, -1),
        kw=np.asarray(L0_cond_k_norm_w).reshape(1, -1), inv_freq=inv_freq.reshape(1, -1),
        w1T=chunked(np.asarray(L1_cond_W).T), aT=chunked(a_all.T),
        bT=np.asarray(L1_cond_B).transpose(0, 2, 1).reshape(ER, HID))

    nc = bacc.Bacc("TRN2", target_bir_lowering=False, num_devices=1)
    arrays, args = {}, {}
    for name, a in ins.items():
        a = np.ascontiguousarray(a)
        arrays[f"in_{name}"] = a
        args[name] = nc.dram_tensor(f"in_{name}", a.shape, mybir.dt.from_np(a.dtype), kind="ExternalInput").ap()
    out = nc.dram_tensor("out_0", (BATCH, SEQ, HID), F32, kind="ExternalOutput").ap()
    y_dram = nc.dram_tensor("y_running", (BATCH * SEQ, HID), F32, kind="Internal").ap()
    program(nc, out=out, y_dram=y_dram, **args)
    r = run_bass_kernel_spmd(nc, [arrays], core_ids=[0])
    return r.results[0]["out_0"]
```

```python
from contextlib import ExitStack

import concourse.bass as bass
from concourse import mybir

ALU = mybir.AluOpType
ACT = mybir.ActivationFunctionType
AX = mybir.AxisListType
F32 = mybir.dt.float32
F32R = mybir.dt.float32r
I32 = mybir.dt.int32
BF16 = mybir.dt.bfloat16

P = 128
BATCH, SEQ, HID = 32, 32, 512
D, HQ, HK = 128, 32, 8
PAGES, PSIZE, NPP = 64, 32, 16
L = NPP * PSIZE
REP = HQ // HK
GK = 2
GROUPS = HK // GK
TILES = BATCH * SEQ // P
ROWS = P // SEQ
PAIRS = ROWS * GK
KC = HID // P
LC = L // P
PPC = P // PSIZE
KEYS = L + P
SPLITS = 5
NBLK = 3
GQ = GK * REP
TOKENS_CACHED = PAGES * PSIZE
SCALE = 1.0 / float(D) ** 0.5
EPS = 1e-6
BIG = 1e30
E_, R_ = 8, 16
ER = E_ * R_
MAGIC = 12582912.0
TWO_PI_1, TWO_PI_2, TWO_PI_3 = 6.28125, 0.0019350051879882812, 3.019916050561733e-07
PI_LOW = 3.1415925


def walk(eng, body):
    def group(g, final):
        body(g, 0, final)
        with eng.Fori(1, TILES - 2) as t:
            body(g, t, final)
        body(g, TILES - 2, final)
        body(g, TILES - 1, final)

    with eng.Fori(0, GROUPS - 1) as g:
        group(g, False)
    group(GROUPS - 1, True)


def program(nc, xT, x, kv, wqkv, wo, block_table, seqlens, lang, qw, kw, inv_freq, w1T, aT, bT, out, y_dram):
    ctx = ExitStack()
    with ctx:
        sb = lambda n, s, d=F32: ctx.enter_context(nc.sbuf_tensor(n, s, d))
        pb = lambda n, s: ctx.enter_context(nc.psum_tensor(n, s, F32))
        sem = lambda n: ctx.enter_context(nc.semaphore(n))

        w_hi = sb("w_hi", [P, NBLK, KC, 512], F32R)
        w_lo = sb("w_lo", [P, NBLK, KC, 512], F32R)
        wo_hi = sb("wo_hi", [P, GQ, HID], F32R)
        wo_lo = sb("wo_lo", [P, GQ, HID], F32R)
        stage = sb("stage", [P, 2, KC, 512])
        x_raw = sb("x_raw", [P, KC, P])
        x_hi = sb("x_hi", [P, KC, P], F32R)
        x_lo = sb("x_lo", [P, KC, P], F32R)
        raw = sb("raw", [P, 512])
        rope_u = sb("rope_u", [P, 512])
        rope_v = sb("rope_v", [P, 512])
        squares = sb("squares", [P, 512], BF16)
        sumsq = sb("sumsq", [P, NBLK, REP])
        meansq = sb("meansq", [P, REP])
        rstd = sb("rstd", [P, REP])
        q_rot = sb("q_rot", [P, GK, 512])
        k_rot = sb("k_rot", [P, GK * D])
        v_next = sb("v_next", [P, GK * D])
        v_new = sb("v_new", [P, GK * D])
        kT_new = sb("kT_new", [P, GK, ROWS, 2, SEQ], F32R)
        qT_hi = sb("qT_hi", [P, GK, ROWS, REP, SEQ], F32R)
        qT_lo = sb("qT_lo", [P, GK, ROWS, REP, SEQ], F32R)
        kv_rows = sb("kv_rows", [P, ROWS, LC, 2 * GK * D])
        kT_hi = sb("kT_hi", [P, L], F32R)
        kT_lo = sb("kT_lo", [P, L], F32R)
        s_new = sb("s_new", [P, PAIRS, SEQ])
        min_new = sb("min_new", [P, PAIRS])
        scores = sb("scores", [P, ROWS, KEYS])
        min_all = sb("min_all", [P, PAIRS])
        probs = sb("probs", [P, KEYS])
        den = sb("den", [P, PAIRS])
        rden = sb("rden", [P, PAIRS])
        pT = sb("pT", [P, KEYS])
        oT_hi = sb("oT_hi", [P, GQ, P], F32R)
        oT_lo = sb("oT_lo", [P, GQ, P], F32R)
        mask = sb("mask", [P, 2, L])
        y_tile = sb("y_tile", [P, HID])
        ident = sb("ident", [P, P])
        key_index = sb("key_index", [P, L])
        cos = sb("cos", [P, TILES, D // 2])
        sin = sb("sin", [P, TILES, D // 2])
        table = sb("table", [P, 4, D])
        norm_w = sb("norm_w", [P, 2, D])
        warm = sb("warm", [P, 1])
        minus_half = sb("minus_half", [P, REP])
        freq = sb("freq", [P, D // 2])
        seq_i = sb("seq_i", [P, BATCH], I32)
        seq_f = sb("seq_f", [P, BATCH])
        lang_i = sb("lang_i", [P, BATCH], I32)
        lang_f = sb("lang_f", [P, BATCH])
        pos = sb("pos", [P, TILES])
        in_page = sb("in_page", [P, 1])
        lang_t = sb("lang_t", [P, TILES])
        rows_idx = sb("rows_idx", [P, GROUPS, BATCH * LC], I32)
        step_idx = sb("step_idx", [P, ROWS * LC], I32)
        expert = sb("expert", [P, E_])
        mask_w = sb("mask_w", [P, 2, D])

        S = [pb("S0", [P, 512]), pb("S1", [P, 512])]
        KT = pb("KT", [P, L])
        PT = pb("PT", [P, 1024])
        O = pb("O", [P, 512])
        PROJ = pb("PROJ", [P, 512])
        MISC = pb("MISC", [P, 512])

        names = ("consts_in bt_in ident_ready iota_ready setup trig const_ready idx_ready mask_init "
                 "stage0_in stage1_in w_hi_ready w_lo_ready xT_in x_hi_ready x_ready y_init y_in y_added y_stored "
                 "proj_done raw_ready sq_ready ms_ready pow_ready uv_ready sum_ready rot_ready table_ready "
                 "kT_new_done kT_new_hi_ready kT_new_ready q_turned qT_hi_ready qT_ready snew_done snew_ready v_new_ready "
                 "kT_done kT_hi_ready kT_ready s_done mask_ready min_ready exp_done rden_ready probs_ready "
                 "pT_done pT_ready pv_done o_hi_ready o_ready y_done "
                 "l1_w_in l1_y0_in l1_y1_in l1_hi l1_lo l1_turned l1_thi l1_tlo l1_h l1_hcopy l1_g l1_e l1_gh l1_ghT l1_ghThi l1_ghTlo "
                 "l1_base l1_sum l1_out trig_w step_idx_ready warm").split()
        sm = {n: sem(n) for n in names}
        kv_in = [sem(f"kv_in{b}") for b in range(ROWS)]

        CREDIT = 1
        credits = [sm[n] for n in ("o_ready", "y_added", "exp_done", "y_done", "pv_done")]

        y_all = kv_rows[:, 0:2, :, :].rearrange("p a c n -> p (a c) n")
        rest = kv_rows[:, 2:4, :, :].rearrange("p a c n -> p (a c n)")
        h_all = rest[:, 0:TILES * (ER + E_)].rearrange("p (t n) -> p t n", t=TILES)
        gh = rest[:, 1088:1088 + TILES * ER].rearrange("p (t n) -> p t n", t=TILES)
        lg = rest[:, 2112:2176].rearrange("p (t e) -> p t e", t=TILES)
        pair_gt = rest[:, 2176:2688].rearrange("p (t e f) -> p t e f", t=TILES, e=E_)
        pair_eq = rest[:, 2688:3200].rearrange("p (t e f) -> p t e f", t=TILES, e=E_)
        lower = rest[:, 3200:3264].rearrange("p (e f) -> p e f", e=E_)
        rank = rest[:, 3264:3328].rearrange("p (t e) -> p t e", t=TILES)
        gate = rest[:, 3328:3392].rearrange("p (t e) -> p t e", t=TILES)
        top = rest[:, 3392:3400]
        total = rest[:, 3400:3408]
        expo = rest[:, 3408:3472].rearrange("p (t e) -> p t e", t=TILES)

        y_rows = y_dram.rearrange("(t p) n -> t p n", p=P)

        def three_pass(out_ps, lhs, rhs, n, first=0, stop_at=None):
            mm = None
            for c in range(first, first + n):
                (ah, al), (bh, bl) = lhs(c), rhs(c)
                for k, (a, b) in enumerate(((ah, bh), (ah, bl), (al, bh))):
                    mm = nc.tensor.matmul(out_ps, a, b, start=(c == 0 and k == 0), stop=(c == stop_at and k == 2))
            return mm

        wide = [S[0], S[1], KT, PT[:, 0:512], PT[:, 512:1024], O]
        narrow = [PROJ, MISC]
        y_turned = lambda t: lambda c: (wo_hi[:, t, c * P:(c + 1) * P], wo_lo[:, t, c * P:(c + 1) * P])

        BLOCK_AT = (1, 4, 6)
        def parts_of(m):
            if m < NBLK:
                return w_hi[:, m, :, :], w_lo[:, m, :, :]
            return tuple(w[:, (m - NBLK) * KC:(m - NBLK + 1) * KC, :] for w in (wo_hi, wo_lo))

        SPLIT_HI_AT = ((TILES - 2, 2), (TILES - 2, 4), (TILES - 1, 0), (0, 0), (0, 2))
        SPLIT_LO_AT = ((TILES - 2, 4), (TILES - 1, 0), (TILES - 1, 2), (0, 2), (0, 4))
        POOL_SPLITS = 1
        L1_SUB = 10

        block = ctx.enter_context(nc.Block())

        @block.sync
        def _(sp):
            for s in credits:
                sp.sem_inc(s, CREDIT)

            def load_weights(g, k):
                src = wqkv[bass.ds(g * NBLK + k, 1), :, :] if k < NBLK else wo[bass.ds(g * 2 + k - NBLK, 1), :, :]
                half = k % 2
                sp.dma_start(stage[:, half, :, :], src.rearrange("a p n -> p (a n)").rearrange("p (c n) -> p c n", c=KC)
                             ).then_inc(sm["stage1_in" if half else "stage0_in"], 16)

            sp.dma_start(x_raw[:, :, :], xT[0, :, :].rearrange("p (c n) -> p c n", c=KC)).then_inc(sm["xT_in"], 16)
            sp.dma_start(stage[:, 0, :, :], wqkv[0, :, :].rearrange("p (c n) -> p c n", c=KC)).then_inc(sm["stage0_in"], 16)
            sp.dma_start(stage[:, 1, :, :], wqkv[1, :, :].rearrange("p (c n) -> p c n", c=KC)).then_inc(sm["stage1_in"], 16)
            sp.wait_ge(sm["w_lo_ready"], 1)
            sp.dma_start(stage[:, 0, :, :], wqkv[2, :, :].rearrange("p (c n) -> p c n", c=KC)).then_inc(sm["stage0_in"], 16)
            sp.wait_ge(sm["x_ready"], 1)
            sp.dma_start(x_raw[:, :, :], xT[1, :, :].rearrange("p (c n) -> p c n", c=KC)).then_inc(sm["xT_in"], 16)
            for k in (NBLK, NBLK + 1):
                sp.wait_ge(sm["w_lo_ready"], k - 1)
                load_weights(0, k)
            sp.dma_start(y_dram[:, :], x[:, :]).then_inc(sm["y_init"], 16)
            sp.wait_ge(sm["y_init"], 16)

            def body(g, t, final):
                i = g * TILES + t
                sp.dma_start(y_tile[:, :], y_rows[bass.ds(t, 1), :, :].rearrange("a p n -> p (a n)")
                             ).then_inc(sm["y_in"], 16)
                if not (final and isinstance(t, int) and t >= TILES - 2):
                    sp.wait_ge(sm["x_ready"], i + 2)
                    sp.nop(nofuse=True)
                    tn = (t + 2) % TILES if isinstance(t, int) else t + 2
                    sp.dma_start(x_raw[:, :, :], xT[bass.ds(tn, 1), :, :].rearrange("a p n -> p (a n)")
                                 .rearrange("p (c n) -> p c n", c=KC)).then_inc(sm["xT_in"], 16)
                if isinstance(t, int) and t == TILES - 1 and not final:
                    for k in (NBLK, NBLK + 1):
                        sp.wait_ge(sm["w_lo_ready"], (g + 1) * SPLITS + k - 1)
                        sp.nop(nofuse=True)
                        load_weights(g + 1, k)
                if final and isinstance(t, int) and t == TILES - 2:
                    sp.wait_ge(sm["w_lo_ready"], GROUPS * SPLITS)
                    sp.wait_ge(sm["x_ready"], GROUPS * TILES)
                    sp.dma_start(stage[:, 0, :, :], w1T.rearrange("p (c n) -> p c n", c=KC)).then_inc(sm["l1_w_in"], 16)
                    sp.dma_start(stage[:, 1, :, 0:ER + E_], aT.rearrange("p (c n) -> p c n", c=KC)).then_inc(sm["l1_w_in"], 16)
                    sp.dma_start(x_raw[:, :, :], bT.rearrange("p (c n) -> p c n", c=KC)).then_inc(sm["l1_w_in"], 16)
                if isinstance(t, int) and t == TILES - 2 and not final:
                    for k in range(NBLK):
                        sp.wait_ge(sm["w_lo_ready"], (g + 1) * SPLITS + max(k - 1, 0))
                        sp.nop(nofuse=True)
                        load_weights(g + 1, k)
                if final and isinstance(t, int) and t == TILES - 1:
                    for first, n, pairs, loaded in ((0, 4, GK, "l1_y0_in"), (4, 3, 2 * GK, "l1_y1_in")):
                        sp.wait_ge(sm["pv_done"], CREDIT + i * PAIRS + pairs)
                        sp.dma_start(y_all[:, first:first + n, :], y_rows[first:first + n, :, :].rearrange("t p n -> p t n")
                                     ).then_inc(sm[loaded], 16)
                    return
                sp.wait_ge(sm["y_added"], CREDIT + i + 1)
                sp.nop(nofuse=True)
                sp.dma_start(y_rows[bass.ds(t, 1), :, :].rearrange("a p n -> p (a n)"), y_tile[:, :]
                             ).then_inc(sm["y_stored"], 16)
                sp.wait_ge(sm["y_stored"], (i + 1) * 16)
                sp.nop(nofuse=True)

            walk(sp, body)
            out_rows = out.rearrange("b s n -> (b s) n").rearrange("(t p) n -> t p n", p=P)
            for t in range(TILES):
                sp.wait_ge(sm["l1_sum"], t + 1)
                sp.dma_start(out_rows[t, :, :], y_all[:, t, :]).then_inc(sm["l1_out"], 16)
            sp.wait_ge(sm["l1_out"], 16 * TILES)

        @block.tensor
        def _(pe):
            xs = lambda c: (x_hi[:, c, :], x_lo[:, c, :])

            def proj(i, k, part, wcount):
                first, n = part
                if first == 0:
                    if k == 0:
                        pe.wait_ge(sm["x_ready"], i + 1)
                        pe.wait_ge(sm["snew_ready"], i * 2)
                    pe.wait_ge(sm["raw_ready"], i * NBLK + k)
                    pe.wait_ge(sm["w_lo_ready"], wcount + k + 1)
                mm = three_pass(PROJ[:, :], xs, lambda c: (w_hi[:, k, c, :], w_lo[:, k, c, :]), n, first, KC - 1)
                if first + n == KC:
                    mm.then_inc(sm["proj_done"], 1)

            def turn_k(i):
                pe.wait_ge(sm["rot_ready"], i * NBLK + 1)
                for h in range(GK):
                    tr = nc.tensor.transpose(MISC[:, h * P:(h + 1) * P], k_rot[:, h * D:(h + 1) * D], ident[:, :])
                tr.then_inc(sm["kT_new_done"], 1)

            def turn_q(i, h):
                pe.wait_ge(sm["rot_ready"], i * NBLK + 2 + h)
                for r in range(REP):
                    tr = nc.tensor.transpose(S[h][:, r * P:(r + 1) * P], q_rot[:, h, r * D:(r + 1) * D], ident[:, :])
                tr.then_inc(sm["q_turned"], 1)

            def products(out_ps, a, b):
                return three_pass(out_ps, lambda c: a, lambda c: b, 1, 0, 0)

            def q_of(b, h):
                return tuple(q[:, h, b, :, :].rearrange("p r s -> p (r s)") for q in (qT_hi, qT_lo))

            def new_scores(i):
                pe.wait_ge(sm["qT_ready"], i * GK + GK)
                pe.wait_ge(sm["kT_new_ready"], i + 1)
                pe.wait_ge(sm["raw_ready"], i * NBLK + NBLK)
                for b in range(ROWS):
                    for h in range(GK):
                        p = b * GK + h
                        q_hi, q_lo = q_of(b, h)
                        nc.tensor.matmul(PROJ[:, 2 * p * SEQ:2 * (p + 1) * SEQ], q_hi,
                                         kT_new[:, h, b, :, :].rearrange("p z s -> p (z s)"), start=True, stop=False)
                        mm = nc.tensor.matmul(PROJ[:, 2 * p * SEQ:(2 * p + 1) * SEQ], q_lo, kT_new[:, h, b, 0, :],
                                              start=False, stop=True)
                mm.then_inc(sm["snew_done"], 1)

            def turn_kv(i, p):
                b, h = p // GK, p % GK
                pe.wait_ge(kv_in[b], (i + 1) * 16 * LC)
                for c in range(LC):
                    tr = nc.tensor.transpose(KT[:, c * P:(c + 1) * P], kv_rows[:, b, c, h * D:(h + 1) * D], ident[:, :])
                tr.then_inc(sm["kT_done"], 1)

            def score(i, p):
                b, h = p // GK, p % GK
                pe.wait_ge(sm["kT_ready"], i * PAIRS + p + 1)
                products(S[p % 2][:, :], q_of(b, h), (kT_hi[:, :], kT_lo[:, :])).then_inc(sm["s_done"], 1)

            def turn_probs(i, p):
                pe.wait_ge(sm["probs_ready"], i * PAIRS + p + 1)
                for c in range(KEYS // P):
                    tr = nc.tensor.transpose(PT[:, c * P:(c + 1) * P], probs[:, c * P:(c + 1) * P], ident[:, :])
                tr.then_inc(sm["pT_done"], 1)

            def weigh(i, p):
                b, h = p // GK, p % GK
                pe.wait_ge(sm["pT_ready"], i * PAIRS + p + 1)
                pe.wait_ge(sm["o_ready"], CREDIT + i * PAIRS + p)
                if p == 0:
                    pe.wait_ge(sm["v_new_ready"], i + 1)
                for c in range(LC):
                    nc.tensor.matmul(O[:, 0:P], kv_rows[:, b, c, GK * D + h * D:GK * D + (h + 1) * D],
                                     pT[:, c * P:(c + 1) * P], start=c == 0, stop=False)
                nc.tensor.matmul(O[:, 0:P], v_new[:, h * D:(h + 1) * D], pT[:, L:KEYS], start=False, stop=True
                                 ).then_inc(sm["pv_done"], 1)

            def project_out(i, h, wcount, first=0, n=REP):
                if h == 0 and first == 0:
                    pe.wait_ge(sm["y_added"], CREDIT + i)
                    pe.wait_ge(sm["kT_new_ready"], i + 1)
                pe.wait_ge(sm["w_lo_ready"], wcount + h)
                pe.wait_ge(sm["o_ready"], CREDIT + i * PAIRS + PAIRS - GK + h + 1)
                mm = three_pass(MISC[:, :], lambda c: (oT_hi[:, c, :], oT_lo[:, c, :]),
                                lambda c: (wo_hi[:, c, :], wo_lo[:, c, :]), n, h * REP + first, GQ - 1)
                if h == GK - 1:
                    mm.then_inc(sm["y_done"], 1)

            pe.wait_ge(sm["ident_ready"], 2)
            for k in range(NBLK):
                proj(0, k, (0, KC), 0)
                if k == 1:
                    turn_kv(0, 0)
            turn_k(0)
            for h in range(GK):
                turn_q(0, h)
            new_scores(0)

            def body(g, t, final):
                i = g * TILES + t
                end_of_group = isinstance(t, int) and t == TILES - 1
                last = final and end_of_group
                wcount = g * SPLITS + (SPLITS if end_of_group else 0)
                fill = [[(0, 0), (0, 1), (0, 2)], [(0, 3)], [(1, 0), (1, 1)], [(1, 2)], [(1, 3)],
                        [(2, 0), (2, 1)], [(2, 2), (2, 3)], []]

                def project_some(n):
                    for k, c in fill[n] if not last else []:
                        proj(i + 1, k, (c, 1), wcount)

                score(i, 0)
                turn_kv(i, 1)
                project_some(0)
                for p in range(PAIRS - 1):
                    score(i, p + 1)
                    turn_probs(i, p)
                    if p + 2 < PAIRS:
                        turn_kv(i, p + 2)
                    elif not last:
                        turn_kv(i + 1, 0)
                    project_some(p + 1)
                    if not last and p == 4:
                        pe.wait_ge(sm["y_added"], CREDIT + i)
                        turn_k(i + 1)
                    if not last and p == PAIRS - 2:
                        turn_q(i + 1, 0)
                    weigh(i, p)
                turn_probs(i, PAIRS - 1)
                project_out(i, 0, g * SPLITS + NBLK + 1, 0, REP - 1)
                if not last:
                    turn_q(i + 1, 1)
                project_out(i, 0, g * SPLITS + NBLK + 1, REP - 1, 1)
                weigh(i, PAIRS - 1)
                if not last:
                    new_scores(i + 1)
                project_out(i, 1, g * SPLITS + NBLK + 1)

            with pe.Fori(0, GROUPS - 1) as g:
                with pe.Fori(0, TILES - 1) as t:
                    body(g, t, False)
                body(g, TILES - 1, False)
            with pe.Fori(0, TILES - 1) as t:
                body(GROUPS - 1, t, True)
            body(GROUPS - 1, TILES - 1, True)

            def turn_y(t):
                for c in range(KC):
                    tr = nc.tensor.transpose(wide[t % 6][:, c * P:(c + 1) * P], y_all[:, t, c * P:(c + 1) * P], ident[:, :])
                tr.then_inc(sm["l1_turned"], 1)

            def down(t):
                pe.wait_ge(sm["l1_tlo"], t + 1)
                if t >= 2:
                    pe.wait_ge(sm["l1_hcopy"], t - 1)
                three_pass(narrow[t % 2][:, 0:ER + E_], y_turned(t),
                           lambda c: (w_hi[:, 1, c, 0:ER + E_], w_lo[:, 1, c, 0:ER + E_]), KC, 0, KC - 1
                           ).then_inc(sm["l1_h"], 1)

            def dense(t):
                if t >= 6:
                    pe.wait_ge(sm["l1_sum"], t - 5)
                three_pass(wide[t % 6][:, :], y_turned(t), lambda c: (w_hi[:, 0, c, :], w_lo[:, 0, c, :]), KC)

            def turn_gh(t):
                pe.wait_ge(sm["l1_gh"], t + 1)
                if t >= 2:
                    pe.wait_ge(sm["l1_ghTlo"], t - 1)
                nc.tensor.transpose(narrow[t % 2][:, 0:P], gh[:, t, :], ident[:, :]).then_inc(sm["l1_ghT"], 1)

            def up(t):
                pe.wait_ge(sm["l1_ghTlo"], t + 1)
                ah, al = x_hi[:, t % 4, :], x_lo[:, t % 4, :]
                bh, bl = w_hi[:, 2, 0, :], w_lo[:, 2, 0, :]
                nc.tensor.matmul(wide[t % 6][:, :], ah, bh, start=False, stop=False)
                nc.tensor.matmul(wide[t % 6][:, :], ah, bl, start=False, stop=False)
                nc.tensor.matmul(wide[t % 6][:, :], al, bh, start=False, stop=True).then_inc(sm["l1_base"], 1)

            pe.wait_ge(sm["l1_lo"], 3)
            pe.wait_ge(sm["min_ready"], GROUPS * TILES * PAIRS)
            pe.wait_ge(sm["o_ready"], CREDIT + GROUPS * TILES * PAIRS)
            for t in range(TILES):
                if t in (0, 4):
                    pe.wait_ge(sm["l1_y1_in" if t else "l1_y0_in"], 16)
                if t == TILES - 1:
                    pe.wait_ge(sm["y_added"], CREDIT + GROUPS * TILES)
                if t >= 6:
                    pe.wait_ge(sm["l1_tlo"], t - 5)
                turn_y(t)
                if t == 2:
                    pe.wait_ge(sm["y_added"], CREDIT + GROUPS * TILES)
                if t >= 2:
                    down(t - 2)
            down(TILES - 2)
            down(TILES - 1)
            for t in range(4):
                dense(t)
            turn_gh(0)
            turn_gh(1)
            for t in range(TILES):
                if t + 4 < TILES:
                    dense(t + 4)
                up(t)
                if t + 2 < TILES:
                    turn_gh(t + 2)

        @block.scalar
        def _(act):
            act.dma_start(freq[:, :], inv_freq.to_broadcast([P, D // 2])).then_inc(sm["consts_in"], 16)
            act.dma_start(seq_i[:, :], seqlens.to_broadcast([P, BATCH])).then_inc(sm["consts_in"], 16)
            act.dma_start(lang_i[:, :], lang.to_broadcast([P, BATCH])).then_inc(sm["consts_in"], 16)
            act.dma_start(norm_w[:, 0, :], qw.to_broadcast([P, D])).then_inc(sm["consts_in"], 16)
            act.dma_start(norm_w[:, 1, :], kw.to_broadcast([P, D])).then_inc(sm["consts_in"], 16)
            act.dma_start(scores.bitcast(I32)[:, 0, 0:BATCH * NPP], block_table.to_broadcast([P, BATCH * NPP])
                          ).then_inc(sm["bt_in"], 16)

            def sines(n, ts):
                act.wait_ge(sm["trig"], 2 * n + 1)
                nc.scalar.activation(sin[:, ts, :], sin[:, ts, :], ACT.Sin).then_inc(sm["const_ready"], 1)
                act.wait_ge(sm["trig"], 2 * n + 2)
                nc.scalar.activation(cos[:, ts, :], cos[:, ts, :], ACT.Sin).then_inc(sm["const_ready"], 1)

            def take_block(i, k):
                act.wait_ge(sm["sq_ready"], i * NBLK + k)
                act.wait_ge(sm["proj_done"], i * NBLK + k + 1)
                act.wait_ge(sm["uv_ready"], i * NBLK + k)
                if k == 0:
                    nc.scalar.activation(raw[:, 0:GK * D], PROJ[:, 0:GK * D], ACT.Copy)
                    act.wait_ge(sm["v_new_ready"], i)
                    nc.scalar.activation(v_next[:, :], PROJ[:, GK * D:512], ACT.Copy).then_inc(sm["raw_ready"], 1)
                else:
                    nc.scalar.activation(raw[:, :], PROJ[:, :], ACT.Copy).then_inc(sm["raw_ready"], 1)

            def square_block(i, k):
                act.wait_ge(sm["raw_ready"], i * NBLK + k + 1)
                act.wait_ge(sm["ms_ready"], i * NBLK + k)
                n = GK if k == 0 else REP
                for r in range(n):
                    sq = nc.scalar.activation(squares[:, r * D:(r + 1) * D], raw[:, r * D:(r + 1) * D], ACT.Square,
                                              accum_out=sumsq[:, k, r:r + 1])
                sq.then_inc(sm["sq_ready"], 1)

            def take_kT_new(i):
                act.wait_ge(sm["kT_new_done"], i + 1)
                nc.scalar.activation(kT_new[:, :, :, 0, :], MISC[:, 0:GK * P].rearrange("p (h b s) -> p h b s", h=GK, b=ROWS),
                                     ACT.Copy).then_inc(sm["kT_new_hi_ready"], 1)

            def take_qT(i, h):
                act.wait_ge(sm["q_turned"], i * GK + h + 1)
                nc.scalar.activation(qT_hi[:, h, :, :, :].rearrange("p b r s -> p r b s"),
                                     S[h][:, :].rearrange("p (r b s) -> p r b s", r=REP, b=ROWS), ACT.Copy
                                     ).then_inc(sm["qT_hi_ready"], 1)

            def take_kT(i, p):
                act.wait_ge(sm["kT_done"], i * PAIRS + p + 1)
                nc.scalar.activation(kT_hi[:, :], KT[:, :], ACT.Copy).then_inc(sm["kT_hi_ready"], 1)

            def take_pT(i, p):
                act.wait_ge(sm["pT_done"], i * PAIRS + p + 1)
                nc.scalar.activation(pT[:, :], PT[:, 0:KEYS], ACT.Copy).then_inc(sm["pT_ready"], 1)

            def exponent(i, p):
                act.wait_ge(sm["min_ready"], i * PAIRS + p + 1)
                nc.scalar.activation(probs[:, :], scores[:, p // GK, :], ACT.Exp, bias=min_all[:, p:p + 1],
                                     scale=-1.0, accum_out=den[:, p:p + 1]).then_inc(sm["exp_done"], 1)

            def round_group_weights(g, t, p, final):
                for m in range(SPLITS):
                    own = m >= NBLK
                    first = SPLIT_HI_AT[m]
                    if (t, p) not in (first, (first[0], first[1] + 1)) or (final and not own):
                        continue
                    part = p - first[1]
                    half = m % 2
                    group = g if own else g + 1
                    if part == 0:
                        if own:
                            act.wait_ge(sm["y_done"], CREDIT + g * TILES)
                        else:
                            act.wait_ge(sm["proj_done"], (g + 1) * TILES * NBLK - NBLK + m + 1)
                        if half:
                            act.wait_ge(sm["stage1_in"], (group * 2 + 1 + m // 2) * 16)
                        else:
                            act.wait_ge(sm["stage0_in"], (group * 3 + 1 + m // 2) * 16)
                    hi, _ = parts_of(m)
                    for c in (2 * part, 2 * part + 1):
                        ins = nc.scalar.activation(hi[:, c, :], stage[:, half, c, :], ACT.Copy)
                    if part == 1:
                        ins.then_inc(sm["w_hi_ready"], 1)

            for k in range(NBLK):
                take_block(0, k)
                square_block(0, k)
                if k == 0:
                    sines(0, slice(0, 1))
                if k == 1:
                    take_kT(0, 0)
            take_kT_new(0)
            for h in range(GK):
                take_qT(0, h)
            sines(1, slice(1, TILES))
            act.wait_ge(sm["setup"], 3)
            nc.scalar.activation(warm[:, :], minus_half[:, 0:1], ACT.Exp).then_inc(sm["warm"], 1)

            def body(g, t, final):
                i = g * TILES + t
                last = final and isinstance(t, int) and t == TILES - 1
                take_kT(i, 1)
                exponent(i, 0)
                for p in range(PAIRS - 1):
                    if not last and p in BLOCK_AT:
                        take_block(i + 1, BLOCK_AT.index(p))
                        square_block(i + 1, BLOCK_AT.index(p))
                    take_pT(i, p)
                    if p + 2 < PAIRS:
                        take_kT(i, p + 2)
                    exponent(i, p + 1)
                    if p + 2 == PAIRS and not last:
                        take_kT(i + 1, 0)
                    if not last and p == 4:
                        take_kT_new(i + 1)
                    if isinstance(t, int):
                        round_group_weights(g, t, p, final)
                take_pT(i, PAIRS - 1)
                if not last:
                    take_qT(i + 1, 0)
                    take_qT(i + 1, 1)

            walk(act, body)

            def take_h(t):
                act.wait_ge(sm["l1_h"], t + 1)
                nc.scalar.activation(h_all[:, t, :], narrow[t % 2][:, 0:ER + E_], ACT.Copy).then_inc(sm["l1_hcopy"], 1)

            for t in range(TILES):
                act.wait_ge(sm["l1_turned"], t + 1)
                if t == 0:
                    act.wait_ge(sm["y_done"], CREDIT + GROUPS * TILES)
                nc.scalar.activation(wo_hi[:, t, :], wide[t % 6][:, :], ACT.Copy).then_inc(sm["l1_thi"], 1)
                if t >= 2:
                    take_h(t - 2)
            take_h(TILES - 2)
            take_h(TILES - 1)
            act.wait_ge(sm["l1_g"], L1_SUB)
            nc.scalar.activation(expo, lg, ACT.Exp).then_inc(sm["l1_e"], 1)
            for t in range(TILES):
                act.wait_ge(sm["l1_ghT"], t + 1)
                nc.scalar.activation(x_hi[:, t % 4, :], narrow[t % 2][:, 0:P], ACT.Copy).then_inc(sm["l1_ghThi"], 1)

        @block.vector
        def _(dve):
            V = nc.vector
            count = [0]

            def setup(ins):
                count[0] += 1
                ins.then_inc(sm["setup"], 1)
                dve.wait_ge(sm["setup"], count[0])

            def round_weights(dst, half, nth):
                dve.wait_ge(sm["stage1_in" if half else "stage0_in"], nth * 16)
                V.tensor_copy(dst, stage[:, half, :, :]).then_inc(sm["w_hi_ready"], 1)

            def rest_weights(k):
                dve.wait_ge(sm["w_hi_ready"], k + 1)
                V.tensor_tensor(w_lo[:, k, :, :], stage[:, 0, :, :], w_hi[:, k, :, :].bitcast(F32), ALU.subtract
                                ).then_inc(sm["w_lo_ready"], 1)

            def rest_group_weights(g, t, p, final, part):
                for m in range(SPLITS):
                    own = m >= NBLK
                    first = SPLIT_LO_AT[m]
                    if (t, p) not in (first, (first[0], first[1] + 1)) or m == POOL_SPLITS or (final and not own):
                        continue
                    half = m % 2
                    group = g if own else g + 1
                    hi, lo = parts_of(m)
                    c = 2 * (p - first[1]) + part
                    if c == 0:
                        dve.wait_ge(sm["w_hi_ready"], group * SPLITS + m + 1)
                        dve.wait_ge(sm["w_lo_ready"], group * SPLITS + m)
                    ins = V.tensor_tensor(lo[:, c, :], stage[:, half, c, :], hi[:, c, :].bitcast(F32), ALU.subtract)
                    if c == KC - 1:
                        ins.then_inc(sm["w_lo_ready"], 1)

            def split_x(i):
                dve.wait_ge(sm["xT_in"], (i + 1) * 16)
                dve.wait_ge(sm["proj_done"], i * NBLK)
                V.tensor_copy(x_hi[:, :, :], x_raw[:, :, :]).then_inc(sm["x_hi_ready"], 1)
                dve.wait_ge(sm["x_hi_ready"], i + 1)
                V.tensor_tensor(x_lo[:, :, :], x_raw[:, :, :], x_hi[:, :, :].bitcast(F32), ALU.subtract
                                ).then_inc(sm["x_ready"], 1)

            def rotate(i, k):
                dve.wait_ge(sm["raw_ready"], i * NBLK + k + 1)
                dve.wait_ge(sm["sum_ready"], i * NBLK + k)
                dve.wait_ge(sm["rot_ready"], i * NBLK + k)
                dve.wait_ge(sm["table_ready"], (i + 1) * 8)
                n, tc = (GK, 2) if k == 0 else (REP, 0)
                w = n * D
                V.tensor_tensor(rope_u[:, 0:w].rearrange("p (r d) -> p r d", d=D), raw[:, 0:w].rearrange("p (r d) -> p r d", d=D),
                                table[:, tc:tc + 1, :].to_broadcast([P, n, D]), ALU.mult)
                r4 = lambda a: a[:, 0:w].rearrange("p (r f d) -> p r f d", r=n, f=2)
                for f in range(2):
                    last = V.tensor_tensor(r4(rope_v)[:, :, f, :], r4(raw)[:, :, 1 - f, :],
                                           table[:, tc + 1:tc + 2, f * 64:(f + 1) * 64].to_broadcast([P, n, 64]), ALU.mult)
                last.then_inc(sm["uv_ready"], 1)

            def take_new_scores(i):
                dve.wait_ge(sm["snew_done"], i + 1)
                V.tensor_reduce(s_new[:, :, :], PROJ[:, :].rearrange("p (a z s) -> p a s z", a=PAIRS, z=2), AX.X, ALU.add
                                ).then_inc(sm["snew_ready"], 1)
                dve.wait_ge(sm["snew_ready"], i * 2 + 1)
                V.tensor_reduce(min_new[:, :], s_new[:, :, :], AX.X, ALU.min).then_inc(sm["snew_ready"], 1)

            def make_mask(row, b):
                V.tensor_scalar(mask[:, b % 2, :], key_index[:, :], seq_f[:, bass.ds(row, 1)], BIG, ALU.is_ge, ALU.mult
                                ).then_inc(sm["mask_ready"], 1)

            def minimum(i, p):
                b = p // GK
                dve.wait_ge(sm["s_done"], i * PAIRS + p + 1)
                dve.wait_ge(sm["exp_done"], CREDIT + i * PAIRS + p)
                if p % GK == 0:
                    dve.wait_ge(sm["mask_ready"], i * ROWS + b + 1)
                if p == 0:
                    dve.wait_ge(sm["snew_ready"], i * 2 + 2)
                dve.nop(nofuse=True)
                V.tensor_copy(scores[:, b, L + b * SEQ:L + (b + 1) * SEQ], s_new[:, p, :])
                V.tensor_tensor_reduce(scores[:, b, 0:L], S[p % 2][:, :], mask[:, b % 2, :], 1.0, min_new[:, p:p + 1],
                                       ALU.add, ALU.min, min_all[:, p:p + 1]).then_inc(sm["min_ready"], 1)

            def normalise(i, p):
                dve.wait_ge(sm["exp_done"], CREDIT + i * PAIRS + p + 1)
                V.reciprocal(rden[:, p:p + 1], den[:, p:p + 1]).then_inc(sm["rden_ready"], 1)
                dve.wait_ge(sm["rden_ready"], i * PAIRS + p + 1)
                V.tensor_scalar(probs[:, :], probs[:, :], rden[:, p:p + 1], None, ALU.mult).then_inc(sm["probs_ready"], 1)

            def take_o(i, p):
                b, h = p // GK, p % GK
                dve.wait_ge(sm["pv_done"], CREDIT + i * PAIRS + p + 1)
                src = O[:, 0:P].rearrange("p (r s) -> p r s", r=REP)
                hi = oT_hi[:, h * REP:(h + 1) * REP, b * SEQ:(b + 1) * SEQ]
                lo = oT_lo[:, h * REP:(h + 1) * REP, b * SEQ:(b + 1) * SEQ]
                V.tensor_copy(hi, src).then_inc(sm["o_hi_ready"], 1)
                dve.wait_ge(sm["o_hi_ready"], i * PAIRS + p + 1)
                V.tensor_tensor(lo, src, hi.bitcast(F32), ALU.subtract).then_inc(sm["o_ready"], 1)

            def rest_kT(i, p):
                dve.wait_ge(sm["kT_hi_ready"], i * PAIRS + p + 1)
                V.tensor_tensor(kT_lo[:, :], KT[:, :], kT_hi[:, :].bitcast(F32), ALU.subtract).then_inc(sm["kT_ready"], 1)

            def rest_kT_new(i):
                dve.wait_ge(sm["kT_new_hi_ready"], i + 1)
                V.tensor_tensor(kT_new[:, :, :, 1, :], MISC[:, 0:GK * P].rearrange("p (h b s) -> p h b s", h=GK, b=ROWS),
                                kT_new[:, :, :, 0, :].bitcast(F32), ALU.subtract).then_inc(sm["kT_new_ready"], 1)

            def rest_qT(i, h):
                dve.wait_ge(sm["qT_hi_ready"], i * GK + h + 1)
                turned = lambda q: q[:, h, :, :, :].rearrange("p b r s -> p r b s")
                V.tensor_tensor(turned(qT_lo), S[h][:, :].rearrange("p (r b s) -> p r b s", r=REP, b=ROWS),
                                turned(qT_hi).bitcast(F32), ALU.subtract).then_inc(sm["qT_ready"], 1)

            def add_y(i, dst):
                dve.wait_ge(sm["y_done"], CREDIT + i + 1)
                dve.wait_ge(sm["y_in"], (i + 1) * 16)
                V.tensor_tensor(dst, y_tile[:, :], MISC[:, :], ALU.add).then_inc(sm["y_added"], 1)

            split_x(0)
            round_weights(w_hi[:, 0, :, :], 0, 1)
            rest_weights(0)
            round_weights(w_hi[:, 1, :, :], 1, 1)
            dve.wait_ge(sm["consts_in"], 80)
            dve.wait_ge(sm["iota_ready"], 3)
            setup(V.tensor_copy(seq_f[:, :], seq_i[:, :]))
            setup(V.tensor_copy(lang_f[:, :], lang_i[:, :]))
            setup(V.memset(minus_half[:, :], -0.5))
            per_row = lambda a, j: a[j * SEQ:(j + 1) * SEQ, :].rearrange("p (t j) -> p t j", j=ROWS)[:, :, j]
            for j in range(ROWS):
                setup(V.tensor_copy(pos[j * SEQ:(j + 1) * SEQ, :], per_row(seq_f, j)))
                setup(V.tensor_copy(lang_t[j * SEQ:(j + 1) * SEQ, :], per_row(lang_f, j)))
                setup(V.tensor_scalar(in_page[j * SEQ:(j + 1) * SEQ, :], in_page[j * SEQ:(j + 1) * SEQ, :],
                                      float(-j * SEQ), None, ALU.add))
            dve.wait_ge(sm["bt_in"], 16)
            pages_i = scores.bitcast(I32)[:, 0, 0:BATCH * NPP]
            pages_f = scores[:, 1, 0:BATCH * NPP]
            base = scores[:, 2, 0:BATCH * LC]
            setup(V.tensor_copy(pages_f, pages_i))
            for j in range(PPC):
                q = slice(j * PSIZE, (j + 1) * PSIZE)
                setup(V.tensor_scalar(base[q, :], pages_f[q, :].rearrange("p (a j) -> p a j", j=PPC)[:, :, j],
                                      float(PSIZE), in_page[q, 0:1], ALU.mult, ALU.add))
            for g in range(GROUPS):
                ins = V.tensor_scalar(rows_idx[:, g, :], base, float(g * TOKENS_CACHED), None, ALU.add)
                ins.then_inc(sm["idx_ready"], 1)
            dve.wait_ge(sm["idx_ready"], GROUPS)
            setup(V.tensor_scalar(pos[:, :], pos[:, :], in_page[:, 0:1], None, ALU.add))
            half_d = D // 2

            def angles(ts, parts=(0, 1)):
                n = ts.stop - ts.start
                ang = scores[:, 0, 0:n * half_d].rearrange("p (t n) -> p t n", t=n)
                turns = scores[:, 1, 0:n * half_d].rearrange("p (t n) -> p t n", t=n)
                if 0 in parts:
                    setup(V.tensor_tensor(ang, pos[:, ts].rearrange("p (t a) -> p t a", a=1).to_broadcast([P, n, half_d]),
                                          freq[:, :].rearrange("p (a n) -> p a n", a=1).to_broadcast([P, n, half_d]),
                                          ALU.mult))
                for part in parts:
                    dst, quarter, add = ((sin, 0.0, 0.0), (cos, 0.25, 1.5707963267948966))[part]
                    d = dst[:, ts, :]
                    setup(V.tensor_scalar(turns, ang, 0.15915494309189535, quarter, ALU.mult, ALU.add))
                    setup(V.tensor_scalar(turns, turns, MAGIC, None, ALU.add))
                    setup(V.tensor_scalar(turns, turns, -MAGIC, None, ALU.add))
                    setup(V.scalar_tensor_tensor(d, turns, -TWO_PI_1, ang, ALU.mult, ALU.add))
                    setup(V.scalar_tensor_tensor(d, turns, -TWO_PI_2, d, ALU.mult, ALU.add))
                    setup(V.scalar_tensor_tensor(d, turns, -TWO_PI_3, d, ALU.mult, ALU.add))
                    setup(V.tensor_scalar(d, d, add, PI_LOW, ALU.add, ALU.min))
                    V.tensor_scalar(d, d, -PI_LOW, None, ALU.max).then_inc(sm["trig"], 1)

            angles(slice(0, 1))
            dve.wait_ge(sm["w_lo_ready"], 1)
            round_weights(w_hi[:, 2, :, :], 0, 2)
            dve.wait_ge(sm["w_lo_ready"], 2)
            rest_weights(2)
            dve.wait_ge(sm["trig"], 2)
            rotate(0, 0)
            rotate(0, 1)
            rest_kT(0, 0)
            angles(slice(1, TILES), (0,))
            rotate(0, 2)
            angles(slice(1, TILES), (1,))
            rest_kT_new(0)
            for h in range(GK):
                rest_qT(0, h)
            dve.wait_ge(sm["trig"], 4)
            V.memset(scores[:, :, L:KEYS], BIG).then_inc(sm["mask_init"], 1)
            dve.wait_ge(sm["mask_init"], 1)
            make_mask(0, 0)
            split_x(1)
            take_new_scores(0)

            def body(g, t, final):
                i = g * TILES + t
                fixed = isinstance(t, int)
                last = final and fixed and t == TILES - 1
                tn = 0 if fixed and t == TILES - 1 else t + 1
                minimum(i, 0)
                rest_kT(i, 1)
                make_mask(t * ROWS + 1, 1)
                normalise(i, 0)
                for p in range(PAIRS - 1):
                    minimum(i, p + 1)
                    if (p + 1) % GK == 0:
                        b = (p + 1) // GK + 1
                        if b < ROWS:
                            make_mask(t * ROWS + b, b)
                        elif not last:
                            make_mask(tn * ROWS, b)
                    if not last and p in BLOCK_AT:
                        rotate(i + 1, BLOCK_AT.index(p))
                    if fixed:
                        rest_group_weights(g, t, p, final, 0)
                    if last and p == 2:
                        dve.wait_ge(sm["l1_w_in"], 48)
                        dve.wait_ge(sm["proj_done"], GROUPS * TILES * NBLK)
                        V.tensor_copy(w_hi[:, 0, :, :], stage[:, 0, :, :]).then_inc(sm["l1_hi"], 1)
                        V.tensor_copy(w_hi[:, 1, :, 0:ER + E_], stage[:, 1, :, 0:ER + E_]).then_inc(sm["l1_hi"], 1)
                        V.tensor_copy(w_hi[:, 2, 0, :], x_raw[:, :, :].rearrange("p c n -> p (c n)")).then_inc(sm["l1_hi"], 1)
                    if p + 2 < PAIRS:
                        rest_kT(i, p + 2)
                    if not last and p == 5:
                        rest_kT_new(i + 1)
                    normalise(i, p + 1)
                    take_o(i, p)
                    if fixed:
                        rest_group_weights(g, t, p, final, 1)
                    if p + 2 == PAIRS and not last:
                        rest_kT(i + 1, 0)
                if not (final and fixed and t >= TILES - 2):
                    split_x(i + 2)
                if not last:
                    for h in range(GK):
                        rest_qT(i + 1, h)
                take_o(i, PAIRS - 1)
                if not last:
                    take_new_scores(i + 1)
                add_y(i, y_all[:, TILES - 1, :] if last else y_tile[:, :])

            walk(dve, body)

            for t in range(TILES):
                dve.wait_ge(sm["l1_thi"], t + 1)
                V.tensor_tensor(wo_lo[:, t, :], wide[t % 6][:, :], wo_hi[:, t, :].bitcast(F32), ALU.subtract
                                ).then_inc(sm["l1_tlo"], 1)
            dve.wait_ge(sm["l1_hcopy"], TILES)
            gs = [0]

            def gating(ins):
                gs[0] += 1
                ins.then_inc(sm["l1_g"], 1)
                dve.wait_ge(sm["l1_g"], gs[0])

            te = [P, TILES, E_]
            tee = [P, TILES, E_, E_]
            ex = expert[:, :]
            gating(V.tensor_tensor(gate, ex.rearrange("p (a e) -> p a e", a=1).to_broadcast(te),
                                   lang_t[:, :].rearrange("p (t a) -> p t a", a=1).to_broadcast(te), ALU.is_equal))
            gating(V.scalar_tensor_tensor(lg, gate, 5.0, h_all[:, :, ER:ER + E_], ALU.mult, ALU.add))
            gating(V.tensor_tensor(lower, ex.rearrange("p (a f) -> p a f", a=1).to_broadcast([P, E_, E_]),
                                   ex.rearrange("p (e a) -> p e a", a=1).to_broadcast([P, E_, E_]), ALU.is_lt))
            other = lg.rearrange("p t (a f) -> p t a f", a=1).to_broadcast(tee)
            own = lg.rearrange("p t (e a) -> p t e a", a=1).to_broadcast(tee)
            gating(V.tensor_tensor(pair_gt, other, own, ALU.is_gt))
            gating(V.tensor_tensor(pair_eq, other, own, ALU.is_equal))
            gating(V.tensor_tensor(pair_eq, pair_eq, lower.rearrange("p (a e) f -> p a e f", a=1).to_broadcast(tee), ALU.mult))
            gating(V.tensor_tensor(pair_gt, pair_gt, pair_eq, ALU.add))
            gating(V.tensor_reduce(rank, pair_gt, AX.X, ALU.add))
            gating(V.tensor_reduce(top, lg, AX.X, ALU.max))
            gating(V.tensor_tensor(lg, lg, top.rearrange("p (t a) -> p t a", a=1).to_broadcast(te), ALU.subtract))
            assert gs[0] == L1_SUB
            dve.wait_ge(sm["l1_e"], 1)
            gating(V.scalar_tensor_tensor(gate, rank, 1.5, expo, ALU.is_lt, ALU.mult))
            gating(V.tensor_reduce(total, gate, AX.X, ALU.add))
            gating(V.reciprocal(total, total))
            gating(V.tensor_scalar(total, total, 2.0, None, ALU.mult))
            gating(V.tensor_tensor(gate, gate, total.rearrange("p (t a) -> p t a", a=1).to_broadcast(te), ALU.mult))
            for t in range(TILES):
                V.tensor_tensor(gh[:, t, :].rearrange("p (e r) -> p e r", e=E_),
                                h_all[:, t, 0:ER].rearrange("p (e r) -> p e r", e=E_),
                                gate[:, t, :].rearrange("p (e a) -> p e a", a=1).to_broadcast([P, E_, R_]), ALU.mult
                                ).then_inc(sm["l1_gh"], 1)
            def rest_ghT(t):
                dve.wait_ge(sm["l1_ghThi"], t + 1)
                V.tensor_tensor(x_lo[:, t % 4, :], narrow[t % 2][:, 0:P], x_hi[:, t % 4, :].bitcast(F32), ALU.subtract
                                ).then_inc(sm["l1_ghTlo"], 1)

            rest_ghT(0)
            rest_ghT(1)
            for t in range(TILES):
                dve.wait_ge(sm["l1_base"], t + 1)
                V.tensor_tensor(y_all[:, t, :], wide[t % 6][:, :], y_all[:, t, :], ALU.add).then_inc(sm["l1_sum"], 1)
                if t + 2 < TILES:
                    rest_ghT(t + 2)

        @block.gpsimd
        def _(pool):
            G = nc.gpsimd
            G.memset(ident[:, :], 0.0).then_inc(sm["ident_ready"], 1)
            pool.wait_ge(sm["ident_ready"], 1)
            G.affine_select(out=ident[:, :], in_=ident[:, :], compare_op=ALU.not_equal, fill=1.0, base=0,
                            pattern=[[-1, P]], channel_multiplier=1).then_inc(sm["ident_ready"], 1)
            G.iota(key_index[:, :], [[1, L]], base=0, channel_multiplier=0, allow_small_or_imprecise_dtypes=True
                   ).then_inc(sm["iota_ready"], 1)
            G.iota(in_page[:, :], [[0, 1]], base=0, channel_multiplier=1, allow_small_or_imprecise_dtypes=True
                   ).then_inc(sm["iota_ready"], 1)
            G.iota(expert[:, :], [[1, E_]], base=0, channel_multiplier=0, allow_small_or_imprecise_dtypes=True
                   ).then_inc(sm["iota_ready"], 1)

            def rest_weights(m, hi, lo, half):
                pool.wait_ge(sm["w_hi_ready"], m + 1)
                G.tensor_tensor(lo, stage[:, half, :, :], hi.bitcast(F32), ALU.subtract).then_inc(sm["w_lo_ready"], 1)

            def gather(b, first, n):
                for c in range(first, first + n):
                    G.indirect_dma_start(kv_rows[:, b, c, :], None, kv[:, :],
                                         bass.IndirectOffsetOnAxis(ap=step_idx[:, b * LC + c:b * LC + c + 1], axis=0)
                                         ).then_inc(kv_in[b], 16)

            def take_indices(i, b0, b1, nth):
                pool.nop(nofuse=True)
                G.tensor_copy(step_idx[:, b0 * LC:b1 * LC], idx_flat[:, bass.ds(i * (ROWS * LC) + b0 * LC, (b1 - b0) * LC)]
                              ).then_inc(sm["step_idx_ready"], 1)
                pool.wait_ge(sm["step_idx_ready"], nth)
                pool.nop(nofuse=True)

            idx_flat = rows_idx[:, :, :].rearrange("p g n -> p (g n)")

            def make_table(i, tn):
                pool.wait_ge(sm["uv_ready"], i * NBLK)
                c, s = (a[:, bass.ds(tn, 1), :].rearrange("p a n -> p (a n)") for a in (cos, sin))
                for z, scale in ((0, -SCALE), (1, 1.0)):
                    for f, sign in ((0, -1.0), (1, 1.0)):
                        cols = slice(f * 64, (f + 1) * 64)
                        other = slice((1 - f) * 64, (2 - f) * 64)
                        G.tensor_tensor(table[:, 2 * z, cols], c, weights[z][:, cols], ALU.mult
                                        ).then_inc(sm["table_ready"], 1)
                        G.tensor_tensor(table[:, 2 * z + 1, cols], s, weights_signed[z][:, other], ALU.mult
                                        ).then_inc(sm["table_ready"], 1)

            weights = [norm_w[:, 0, :], norm_w[:, 1, :]]
            weights_signed = [mask_w[:, 0, :], mask_w[:, 1, :]]

            def make_rstd(i, k):
                n = GK if k == 0 else REP
                nth = i * NBLK + k + 1
                pool.wait_ge(sm["rot_ready"], nth - 1)
                pool.wait_ge(sm["sq_ready"], nth)
                pool.nop(nofuse=True)
                G.tensor_scalar(meansq[:, 0:n], sumsq[:, k, 0:n], 1.0 / D, EPS, ALU.mult, ALU.add
                                ).then_inc(sm["ms_ready"], 1)
                pool.wait_ge(sm["ms_ready"], nth)
                G.tensor_tensor(rstd[:, 0:n], meansq[:, 0:n], minus_half[:, 0:n], ALU.pow).then_inc(sm["pow_ready"], 1)

            def rotate_sum(i, k):
                n = GK if k == 0 else REP
                nth = i * NBLK + k + 1
                pool.wait_ge(sm["uv_ready"], nth)
                pool.nop(nofuse=True)
                w = n * D
                G.tensor_tensor(rope_u[:, 0:w], rope_u[:, 0:w], rope_v[:, 0:w], ALU.add).then_inc(sm["sum_ready"], 1)
                pool.wait_ge(sm["sum_ready"], nth)
                pool.wait_ge(sm["pow_ready"], nth)
                if k == 0:
                    pool.wait_ge(sm["kT_new_done"], i)
                    dst = k_rot[:, :]
                else:
                    pool.wait_ge(sm["q_turned"], i * GK)
                    dst = q_rot[:, k - 1, :]
                G.tensor_tensor(dst.rearrange("p (r d) -> p r d", d=D), rope_u[:, 0:w].rearrange("p (r d) -> p r d", d=D),
                                rstd[:, 0:n].rearrange("p (r a) -> p r a", a=1).to_broadcast([P, n, D]), ALU.mult
                                ).then_inc(sm["rot_ready"], 1)

            def keep_v(i):
                pool.wait_ge(sm["raw_ready"], i * NBLK + 1)
                pool.wait_ge(sm["pv_done"], CREDIT + i * PAIRS)
                pool.nop(nofuse=True)
                G.tensor_copy(v_new[:, :], v_next[:, :]).then_inc(sm["v_new_ready"], 1)

            pool.wait_ge(sm["consts_in"], 80)
            G.tensor_scalar(norm_w[:, 0, :], norm_w[:, 0, :], -SCALE, 0.0, ALU.mult, ALU.add).then_inc(sm["trig_w"], 1)
            pool.wait_ge(sm["trig_w"], 1)
            for z in range(2):
                G.tensor_scalar(mask_w[:, z, 0:64], norm_w[:, z, 0:64], 1.0, 0.0, ALU.mult, ALU.add).then_inc(sm["trig_w"], 1)
                G.tensor_scalar(mask_w[:, z, 64:128], norm_w[:, z, 64:128], -1.0, 0.0, ALU.mult, ALU.add).then_inc(sm["trig_w"], 1)
            pool.wait_ge(sm["trig_w"], 5)
            rest_weights(1, w_hi[:, 1, :, :], w_lo[:, 1, :, :], 1)
            pool.wait_ge(sm["idx_ready"], GROUPS)
            take_indices(0, 0, ROWS - 1, 1)
            gather(0, 0, LC)
            pool.wait_ge(sm["const_ready"], 2)
            make_table(0, 0)
            for k in range(NBLK):
                make_rstd(0, k)
                rotate_sum(0, k)
                if k == 0:
                    gather(1, 0, LC)
            keep_v(0)
            gather(2, 0, LC)
            pool.wait_ge(sm["const_ready"], 4)
            pool.wait_ge(sm["mask_init"], 1)

            def body(g, t, final):
                i = g * TILES + t
                fixed = isinstance(t, int)
                last = final and fixed and t == TILES - 1
                tn = 0 if fixed and t == TILES - 1 else t + 1
                for p in range(PAIRS):
                    if not last and p == 0:
                        make_table(i + 1, tn)
                    if fixed and not final and (t, p) == SPLIT_LO_AT[POOL_SPLITS]:
                        k = POOL_SPLITS
                        rest_weights((g + 1) * SPLITS + k, w_hi[:, k, :, :], w_lo[:, k, :, :], k % 2)
                    if not last and p - 1 in BLOCK_AT:
                        if p < PAIRS - 1:
                            make_rstd(i + 1, BLOCK_AT.index(p - 1))
                        rotate_sum(i + 1, BLOCK_AT.index(p - 1))
                        if p == PAIRS - 1:
                            gather(p // 2 - 1, 1, 1)
                    if p < 2:
                        b = ROWS - 1
                        if p == 0:
                            pool.wait_ge(sm["pv_done"], CREDIT + i * PAIRS)
                            take_indices(i, b, b + 1, 2 * i + 2)
                        gather(b, 2 * p, 2)
                    elif not last:
                        b = p // 2 - 1
                        if p == 2:
                            for row in range(ROWS - 1):
                                pool.wait_ge(kv_in[row], (i + 1) * 16 * LC)
                            take_indices(i + 1, 0, ROWS - 1, 2 * i + 3)
                        pool.wait_ge(sm["pv_done"], CREDIT + i * PAIRS + b * GK + GK)
                        pool.nop(nofuse=True)
                        if p == PAIRS - 2:
                            gather(b, 0, 1)
                            make_rstd(i + 1, NBLK - 1)
                        else:
                            gather(b, 2 * (p % 2), 2)
                    if last and p == 3:
                        pool.wait_ge(sm["l1_hi"], 3)
                        G.tensor_tensor(w_lo[:, 1, :, 0:ER + E_], stage[:, 1, :, 0:ER + E_],
                                        w_hi[:, 1, :, 0:ER + E_].bitcast(F32), ALU.subtract).then_inc(sm["l1_lo"], 1)
                        G.tensor_tensor(w_lo[:, 0, :, :], stage[:, 0, :, :], w_hi[:, 0, :, :].bitcast(F32), ALU.subtract
                                        ).then_inc(sm["l1_lo"], 1)
                        G.tensor_tensor(w_lo[:, 2, 0, :], x_raw[:, :, :].rearrange("p c n -> p (c n)"),
                                        w_hi[:, 2, 0, :].bitcast(F32), ALU.subtract).then_inc(sm["l1_lo"], 1)
                if not last:
                    keep_v(i + 1)

            walk(pool, body)


def kernel(x, itok_Bx16_0_63, itok_B_207_1644, itok_B_0_7, L0_cond_Wq, L0_cond_Wk, L0_cond_Wv, L0_cond_Wo,
           L0_cond_q_norm_w, L0_cond_k_norm_w, L0_cond_k_cache, L0_cond_v_cache, L1_cond_W, L1_cond_Wr, L1_cond_A, L1_cond_B):
    import numpy as np
    import concourse.bacc as bacc
    from concourse.bass_utils import run_bass_kernel_spmd

    def chunked(wT):
        return np.asarray(wT).reshape(KC, P, -1).transpose(1, 0, 2).reshape(P, -1)

    x2 = np.asarray(x).reshape(BATCH * SEQ, HID)
    xT = x2.reshape(TILES, P, KC, P).transpose(0, 3, 2, 1).reshape(TILES, P, KC * P)
    k4 = np.asarray(L0_cond_k_cache).reshape(TOKENS_CACHED, GROUPS, GK * D)
    v4 = np.asarray(L0_cond_v_cache).reshape(TOKENS_CACHED, GROUPS, GK * D)
    kv = np.concatenate([k4, v4], axis=2).transpose(1, 0, 2).reshape(GROUPS * TOKENS_CACHED, 2 * GK * D)
    wq, wk, wv, wo = (np.asarray(a) for a in (L0_cond_Wq, L0_cond_Wk, L0_cond_Wv, L0_cond_Wo))
    blocks = []
    for g in range(GROUPS):
        n = GK * D
        blocks.append(chunked(np.concatenate([wk[g * n:(g + 1) * n], wv[g * n:(g + 1) * n]], axis=0).T))
        for h in range(GK):
            r = (g * GK + h) * REP * D
            blocks.append(chunked(wq[r:r + REP * D].T))
    wo_l = wo.T.reshape(GROUPS * 2, REP, D, HID).transpose(0, 2, 1, 3).reshape(GROUPS * 2, D, REP * HID)
    a_all = np.concatenate([np.asarray(L1_cond_A).reshape(ER, HID), np.asarray(L1_cond_Wr)], axis=0)
    exponents = np.arange(0, D, 2, dtype=np.float32) / np.float32(D)
    inv_freq = np.float32(1.0) / np.power(10000.0, exponents.astype(np.float64)).astype(np.float32)
    ins = dict(
        xT=xT, x=x2, kv=kv, wqkv=np.stack(blocks), wo=wo_l,
        block_table=np.asarray(itok_Bx16_0_63).reshape(1, -1), seqlens=np.asarray(itok_B_207_1644).reshape(1, -1),
        lang=np.asarray(itok_B_0_7).reshape(1, -1), qw=np.asarray(L0_cond_q_norm_w).reshape(1, -1),
        kw=np.asarray(L0_cond_k_norm_w).reshape(1, -1), inv_freq=inv_freq.reshape(1, -1),
        w1T=chunked(np.asarray(L1_cond_W).T), aT=chunked(a_all.T),
        bT=np.asarray(L1_cond_B).transpose(0, 2, 1).reshape(ER, HID))

    nc = bacc.Bacc("TRN2", target_bir_lowering=False, num_devices=1)
    arrays, args = {}, {}
    for name, a in ins.items():
        a = np.ascontiguousarray(a)
        arrays[f"in_{name}"] = a
        args[name] = nc.dram_tensor(f"in_{name}", a.shape, mybir.dt.from_np(a.dtype), kind="ExternalInput").ap()
    out = nc.dram_tensor("out_0", (BATCH, SEQ, HID), F32, kind="ExternalOutput").ap()
    y_dram = nc.dram_tensor("y_running", (BATCH * SEQ, HID), F32, kind="Internal").ap()
    program(nc, out=out, y_dram=y_dram, **args)
    r = run_bass_kernel_spmd(nc, [arrays], core_ids=[0])
    return r.results[0]["out_0"]
```
